# Optimizing a Trainium2 kernel written in Bass

```python
import numpy as np
import jax
import jax.numpy as jnp

def _softmax(x, axis=-1):
    return jax.nn.softmax(x, axis=axis)

def _gelu(x):
    return jax.nn.gelu(x, approximate=True)

def _silu(x):
    return jax.nn.silu(x)

def _sigmoid(x):
    return jax.nn.sigmoid(x)

def _layernorm(x, axis=-1, eps=1e-05):
    m = jnp.mean(x, axis=axis, keepdims=True)
    v = jnp.var(x, axis=axis, keepdims=True)
    return (x - m) / jnp.sqrt(v + eps)

def _scatter_add(tgt, idx, src, axis=0):
    return tgt.at[idx].add(src)

def _segment_sum(src, seg, n):
    return jax.ops.segment_sum(src, seg, n)
kernel_name = 'mk_cond_resid_d4_seqx_r2_d25dea'

def setup_inputs(seed: int=0):
    np.random.seed(seed)
    _w = jnp.asarray

    def _rec_inputs():
        import jax
        import jax.numpy as jnp
        _rk = jax.random.key(seed)
        x = 0.5 + 0.2887 * jax.random.normal(jax.random.fold_in(_rk, 1), (8, 1024, 512), jnp.float32)
        _lenS = 1024 - jax.random.randint(jax.random.fold_in(_rk, 7), (8,), 0, max(1, 1024 // 4) + 1, jnp.int32)
        _lenS2 = 1024 - jax.random.randint(jax.random.fold_in(_rk, 8), (8,), 0, max(1, 1024 // 4) + 1, jnp.int32)
        condB_zX = jax.random.uniform(jax.random.fold_in(_rk, 11), (8,), jnp.float32, 0.0, 0.983423)
        condB_zY = jax.random.uniform(jax.random.fold_in(_rk, 12), (8,), jnp.float32, 0.0, 0.979075)
        condB_zR = jax.random.uniform(jax.random.fold_in(_rk, 13), (8,), jnp.float32, 0.0, 0.9968)
        itok_B_0_2 = jax.random.randint(jax.random.fold_in(_rk, 14), (8,), 0, 3, jnp.int32)
        itok_B_0_7 = jax.random.randint(jax.random.fold_in(_rk, 15), (8,), 0, 8, jnp.int32)
        itok_B_0_6 = jax.random.randint(jax.random.fold_in(_rk, 16), (8,), 0, 7, jnp.int32)
        return (x, condB_zX, condB_zY, condB_zR, itok_B_0_2, itok_B_0_7, itok_B_0_6)
    x, condB_zX, condB_zY, condB_zR, itok_B_0_2, itok_B_0_7, itok_B_0_6 = _rec_inputs()

    def _L0_cond_setup():
        import jax, jax.numpy as jnp
        import numpy as np
        key = jax.random.key(seed)
        k1, k2, k3, k4 = jax.random.split(key, 4)
        B, H, W = (64, 512, 512)
        return {'y': jax.random.uniform(k1, (B, H, W), dtype=jnp.float32), 'zX': jax.random.uniform(k2, (B, 1), dtype=jnp.float32), 'zY': jax.random.uniform(k3, (B, 1), dtype=jnp.float32), 'zR': jax.random.uniform(k4, (B, 1), dtype=jnp.float32), 'dx': 1, 'dy': 1}
    _L0_cond_all = _L0_cond_setup()
    _L0_cond_in = {k: v for k, v in _L0_cond_all.items() if k in ()}
    del _L0_cond_all

    def _L1_cond_setup():
        import jax, jax.numpy as jnp
        import numpy as np
        NEG_INF = -1e+30
        key = jax.random.key(seed)
        k1, k2, k3, k4, k5 = jax.random.split(key, 5)
        B, S, D, A = (16, 512, 512, 128)
        hidden = jax.random.normal(k1, (B, S, D), dtype=jnp.float32)
        W1 = jax.random.normal(k2, (D, A), dtype=jnp.float32) / np.sqrt(D)
        b1 = jax.random.normal(k3, (A,), dtype=jnp.float32) * 0.01
        v = jax.random.normal(k4, (A,), dtype=jnp.float32) / np.sqrt(A)
        prompt_type_ids = jax.random.randint(k5, (B,), 0, 3, dtype=jnp.int32)
        return {'hidden': hidden, 'W1': W1, 'b1': b1, 'v': v, 'prompt_type_ids': prompt_type_ids}
    _L1_cond_all = _L1_cond_setup()
    _L1_cond_in = {k: v for k, v in _L1_cond_all.items() if k in ('W1', 'b1', 'v')}
    del _L1_cond_all

    def _L2_cond_setup():
        import jax, jax.numpy as jnp
        import numpy as np
        S, O, H = (8, 512, 512)
        B, N = (32, 256)
        key = jax.random.key(seed)
        k1, k2, k3, k4 = jax.random.split(key, 4)
        x = jax.random.normal(k1, (B, N, H), dtype=jnp.float32)
        subject_id = jax.random.randint(k2, (B,), 0, S)
        wbound = jnp.sqrt(2.0 / 6.0) * jnp.sqrt(3.0 / H)
        weight = jax.random.uniform(k3, (S, O, H), minval=-wbound, maxval=wbound, dtype=jnp.float32)
        bbound = 1.0 / jnp.sqrt(H)
        bias = jax.random.uniform(k4, (S, O), minval=-bbound, maxval=bbound, dtype=jnp.float32)
        return {'x': x, 'subject_id': subject_id, 'weight': weight, 'bias': bias}
    _L2_cond_all = _L2_cond_setup()
    _L2_cond_in = {k: v for k, v in _L2_cond_all.items() if k in ('weight', 'bias')}
    del _L2_cond_all

    def _L3_cond_setup():
        import jax, jax.numpy as jnp
        import numpy as np
        N_PROFILES = 8
        HIDDEN = 512
        BOTTLENECK = 128
        EPS = 1e-05
        key = jax.random.key(seed)
        ks = jax.random.split(key, 8)
        B, S, H, K, P = (16, 1024, HIDDEN, BOTTLENECK, N_PROFILES)
        down_w = jax.random.normal(ks[0], (P, H, K), dtype=jnp.float32) * (1.0 / np.sqrt(H))
        down_b = jax.random.normal(ks[1], (P, K), dtype=jnp.float32) * 0.01
        up_w = jax.random.normal(ks[2], (P, K, H), dtype=jnp.float32) * (1.0 / np.sqrt(K))
        up_b = jax.random.normal(ks[3], (P, H), dtype=jnp.float32) * 0.01
        ln_g = jnp.ones((P, H), dtype=jnp.float32)
        ln_b = jnp.zeros((P, H), dtype=jnp.float32)
        hidden = jax.random.normal(ks[4], (B, S, H), dtype=jnp.float32)
        profile_ids = jax.random.randint(ks[5], (B,), 0, P)
        return {'hidden': hidden, 'profile_ids': profile_ids, 'down_w': down_w, 'down_b': down_b, 'up_w': up_w, 'up_b': up_b, 'ln_g': ln_g, 'ln_b': ln_b}
    _L3_cond_all = _L3_cond_setup()
    _L3_cond_in = {k: v for k, v in _L3_cond_all.items() if k in ('down_w', 'down_b', 'up_w', 'up_b', 'ln_g', 'ln_b')}
    del _L3_cond_all
    return {'x': x, 'condB_zX': condB_zX, 'condB_zY': condB_zY, 'condB_zR': condB_zR, 'itok_B_0_2': itok_B_0_2, 'itok_B_0_7': itok_B_0_7, 'itok_B_0_6': itok_B_0_6, 'L1_cond_W1': _L1_cond_in['W1'], 'L1_cond_b1': _L1_cond_in['b1'], 'L1_cond_v': _L1_cond_in['v'], 'L2_cond_weight': _L2_cond_in['weight'], 'L2_cond_bias': _L2_cond_in['bias'], 'L3_cond_down_w': _L3_cond_in['down_w'], 'L3_cond_down_b': _L3_cond_in['down_b'], 'L3_cond_up_w': _L3_cond_in['up_w'], 'L3_cond_up_b': _L3_cond_in['up_b'], 'L3_cond_ln_g': _L3_cond_in['ln_g'], 'L3_cond_ln_b': _L3_cond_in['ln_b']}

def reference(x, condB_zX, condB_zY, condB_zR, itok_B_0_2, itok_B_0_7, itok_B_0_6, L1_cond_W1, L1_cond_b1, L1_cond_v, L2_cond_weight, L2_cond_bias, L3_cond_down_w, L3_cond_down_b, L3_cond_up_w, L3_cond_up_b, L3_cond_ln_g, L3_cond_ln_b):
    import jax
    import jax.numpy as jnp

    def _L0_cond_ref(y, zX, zY, zR, dx, dy):
        import jax, jax.numpy as jnp
        import numpy as np
        yp_x = jnp.pad(y, ((0, 0), (0, 0), (1, 1)), mode='reflect')
        lap_x = (yp_x[:, :, :-2] - 2.0 * y + yp_x[:, :, 2:]) / (dx * dx)
        yp_y = jnp.pad(y, ((0, 0), (1, 1), (0, 0)), mode='reflect')
        lap_y = (yp_y[:, :-2, :] - 2.0 * y + yp_y[:, 2:, :]) / (dy * dy)
        du_dt = zX[:, :, None] * lap_x + zY[:, :, None] * lap_y + zR[:, :, None] * y * (1.0 - y)
        return du_dt

    def _L1_cond_ref(hidden, W1, b1, v, prompt_type_ids):
        import jax, jax.numpy as jnp
        import numpy as np
        NEG_INF = -1e+30
        B, S, D = hidden.shape
        attn_in = jnp.tanh(jnp.einsum('bsd,da->bsa', hidden, W1) + b1)
        scores = jnp.einsum('bsa,a->bs', attn_in, v)
        idx = jnp.arange(S)
        j = idx[:, None]
        l = idx[None, :]
        prefix_m = l <= j
        postfix_m = l >= j
        cloze_m = l != j
        pt = prompt_type_ids[:, None, None]
        mask = jnp.where(pt == 0, prefix_m[None], jnp.where(pt == 1, postfix_m[None], cloze_m[None]))
        masked_scores = jnp.where(mask, scores[:, None, :], NEG_INF)
        p = jax.nn.softmax(masked_scores, axis=-1)
        cnt = jnp.sum(mask, axis=-1).astype(hidden.dtype)
        pooled = jnp.einsum('bjl,bld->bjd', p, hidden) / cnt[..., None]
        return pooled

    def _L2_cond_ref(x, subject_id, weight, bias):
        import jax, jax.numpy as jnp
        import numpy as np
        S, O, H = (8, 512, 512)
        B, N = (32, 256)
        W = weight[subject_id]
        b = bias[subject_id]
        y = jnp.einsum('bnh,boh->bno', x, W) + b[:, None, :]
        return y

    def _L3_cond_ref(hidden, profile_ids, down_w, down_b, up_w, up_b, ln_g, ln_b):
        import jax, jax.numpy as jnp
        import numpy as np
        N_PROFILES = 8
        HIDDEN = 512
        BOTTLENECK = 128
        EPS = 1e-05
        Wd = down_w[profile_ids]
        bd = down_b[profile_ids][:, None]
        Wu = up_w[profile_ids]
        bu = up_b[profile_ids][:, None]
        g = ln_g[profile_ids][:, None]
        b = ln_b[profile_ids][:, None]
        z = jax.nn.relu(jnp.einsum('bsh,bhk->bsk', hidden, Wd) + bd)
        y = hidden + jnp.einsum('bsk,bkh->bsh', z, Wu) + bu
        mu = jnp.mean(y, axis=-1, keepdims=True)
        var = jnp.mean(jnp.square(y - mu), axis=-1, keepdims=True)
        return (y - mu) * jax.lax.rsqrt(var + EPS) * g + b
    x = x + _L0_cond_ref(x, condB_zX[:, None], condB_zY[:, None], condB_zR[:, None], 1, 1)
    x = x + _L1_cond_ref(x, L1_cond_W1, L1_cond_b1, L1_cond_v, itok_B_0_2)
    x = x + _L2_cond_ref(x, itok_B_0_7, L2_cond_weight, L2_cond_bias)
    x = x + _L3_cond_ref(x, itok_B_0_6, L3_cond_down_w, L3_cond_down_b, L3_cond_up_w, L3_cond_up_b, L3_cond_ln_g, L3_cond_ln_b)
    return x

_drawn_inputs = setup_inputs


def setup_inputs(seed=0):
    import zlib

    import numpy as np

    out = dict(_drawn_inputs(seed))
    spreads = {'L3_cond_ln_g': (1.0, 0.2), 'L3_cond_ln_b': (0.0, 0.1)}
    factors = {'L1_cond_W1': 8.0,
     'L1_cond_b1': 8.0,
     'L1_cond_v': 8.0,
     'L3_cond_down_b': 8.0,
     'L3_cond_up_b': 7.821}
    for name, (base, spread) in spreads.items():
        noise = np.random.default_rng([zlib.crc32(name.encode()), seed]).standard_normal(out[name].shape)
        drawn = base * np.exp(spread * noise) if base else spread * noise
        out[name] = jnp.asarray(drawn.astype(out[name].dtype))
    for name, factor in factors.items():
        out[name] = (out[name] * factor).astype(out[name].dtype)
    return out
```

```python
from contextlib import ExitStack

import numpy as np
import concourse.bass as bass
from concourse import mybir

F32 = mybir.dt.float32
F32R = mybir.dt.float32r
I32 = mybir.dt.int32
ALU = mybir.AluOpType
ACT = mybir.ActivationFunctionType
AX = mybir.AxisListType

P = 128
BIG = -1.0e30
EPS = 1e-5
TABLE = 7
Z_X, Z_Y, CENTRE, MINUS_R, IS_PREFIX, IS_POSTFIX, IS_CLOZE = range(7)


def wait_past(eng, sem, count):
    if isinstance(count, int) and count <= 0:
        return
    eng.wait_ge(sem, count)


class Chain:

    def __init__(self, sem, per_batch):
        self.sem, self.per_batch, self.n, self.base = sem, per_batch, 0, 0

    def start(self, batch):
        self.n, self.base = 0, batch * self.per_batch

    def mark(self, ins):
        ins.then_inc(self.sem, 1)
        self.n += 1
        return self.n

    def wait(self, eng, n=None):
        eng.wait_ge(self.sem, self.base + (self.n if n is None else n))

    def end(self):
        assert self.n == self.per_batch, (self.n, self.per_batch)


def build(nc, x, condB_zX, condB_zY, condB_zR, itok_B_0_2, itok_B_0_7, itok_B_0_6,
          L1_W1, L1_b1, L1_v, L2_w, L2_b, L3_dw, L3_db, L3_uw, L3_ub, L3_g, L3_b, out):
    B, S, D = x.shape
    A = L1_W1.shape[1]
    NJ = S // P
    KD = D // P
    NC = NJ // 2
    NSUB, NPROF = L2_w.shape[0], L3_dw.shape[0]
    assert A == P and NJ == 8 and KD == 4
    HALF = S // 2
    NB = NJ * NJ
    MASK = P + NB + NJ
    YB, XB, TB, OB = 3, 3, 2, 4

    with ExitStack() as ctx:
        def sb(name, shape, dt=F32):
            return ctx.enter_context(nc.sbuf_tensor(name, shape, dt))

        def ps(name, cols):
            return ctx.enter_context(nc.psum_tensor(name, [P, cols], F32))

        def sem(name):
            return ctx.enter_context(nc.semaphore(name))

        ident = sb("ident", [P, P])
        masks = sb("masks", [P, 3, MASK])
        bias_rows_f = sb("bias_rows_f", [P, P])
        bias_rows_on = sb("bias_rows_on", [P, P], F32R)
        ones = sb("ones", [P, P])
        v_rep = sb("v_rep", [P, P])
        v_col = sb("v_col", [P, 1])
        b1_col = sb("b1_col", [P, 1])
        w1 = sb("w1", [P, KD, A])
        minus_half = sb("minus_half", [P, 1])
        raw3 = sb("raw3", [P, 3, B])
        iota_i = sb("iota_i", [P, NJ], I32)
        tok_i = sb("tok_i", [P, B], I32)
        tok_f = sb("tok_f", [P, B])
        table = sb("table", [P, TABLE, B])
        xn = sb("xn", [P, 2, 2, D + 2])
        xu = sb("xu", [P, 2, 2, D])
        xd = sb("xd", [P, 2, 2, D])
        x1 = sb("x1", [P, NJ, D])
        x1t = sb("x1t", [P, KD, S])
        cur = sb("cur", [P, TABLE])
        mask = sb("mask", [P, MASK])
        th = sb("th", [P, S])
        pn = sb("pn", [P, S])
        pt = sb("pt", [P, S])
        alb = sb("alb", [P, S])
        small = sb("small", [P, 512])
        prod = sb("prod", [P, KD + 1, NJ, NJ])
        x2f = sb("x2f", [P, 2, S])
        x2h = sb("x2h", [P, KD, S], F32R)
        x2l = sb("x2l", [P, KD, S], F32R)
        wn = sb("wn", [P, KD, D])
        wth = sb("wth", [P, KD, D], F32R)
        wtl = sb("wtl", [P, KD, D], F32R)
        wd = sb("wd", [P, KD, P])
        vh = sb("vh", [P, KD, P], F32R)
        vl = sb("vl", [P, KD, P], F32R)
        wu = sb("wu", [P, D])
        wuh = sb("wuh", [P, D], F32R)
        wul = sb("wul", [P, D], F32R)
        b_col = sb("b_col", [P, KD])
        bd_col = sb("bd_col", [P, 1])
        bz = sb("bz", [P, 1])
        rows = sb("rows", [P, 3, D])
        row_sum = sb("row_sum", [P, 2, D])
        bias = sb("bias", [P, 2, D], F32R)
        g_in = sb("g_in", [P, D])
        g_row = sb("g_row", [P, D])
        zf = sb("zf", [P, S])
        zh = sb("zh", [P, S], F32R)
        zl = sb("zl", [P, S], F32R)
        x3 = sb("x3", [P, XB, D])
        t1 = sb("t1", [P, TB, D])
        o_sb = sb("o_sb", [P, OB, D])
        stats = sb("stats", [P, TB, 6])
        mv = sb("mv", [P, TB, 2])
        ve = sb("ve", [P, TB])
        rstd = sb("rstd", [P, TB])
        carrier = sb("carrier", [P, 1])

        ys = [ps(f"y{i}", D) for i in range(YB)]
        pair_a, pair_b = ps("pair_a", S), ps("pair_b", S)
        cbank = ps("cbank", 512)
        SN, ZG, BZ = cbank[:, 0:NJ], 8, 64

        off = [0]

        def cols(n):
            off[0] += n
            return small[:, off[0] - n:off[0]]

        MI = cols(NJ)
        MDIAG, MCAR, M, NEGM = cols(NJ), cols(NJ), cols(NJ), cols(NJ)
        KM = cols(NB)
        ARG = cols(2 * NJ + NB)
        EX = cols(2 * NJ + NB)
        E_ROW, KAP, ALH = EX[:, 0:NJ], EX[:, NJ:NJ + NB], EX[:, NJ + NB:]
        ZD, CC, ZT, RZ, AL = cols(NJ), cols((KD + 1) * NJ), cols(NJ), cols(NJ), cols(NJ)
        ZT2 = cols(NJ)

        const_in = sem("const_in")
        const_made = sem("const_made")
        table_made = sem("table_made")
        cur_ready = sem("cur_ready")
        wt_loaded = sem("wt_loaded")
        row_loaded = sem("row_loaded")
        up_loaded = sem("up_loaded")
        halo = sem("halo")
        c_done = sem("c_done")
        pool_a = sem("pool_a")
        pool_b = sem("pool_b")
        l0_done = sem("l0_done")
        xt_ps = sem("xt_ps")
        x1t_ready = sem("x1t_ready")
        h_ps = sem("h_ps")
        th_ready = sem("th_ready")
        sc_ps = sem("sc_ps")
        sn_ps = sem("sn_ps")
        sb_read = sem("sb_read")
        arg_ready = sem("arg_ready")
        ex_ready = sem("ex_ready")
        negm_ready = sem("negm_ready")
        p_exp = sem("p_exp")
        g_ps = sem("g_ps")
        cc_ready = sem("cc_ready")
        al_ready = sem("al_ready")
        pn_ready = sem("pn_ready")
        al_ps = sem("al_ps")
        pt_ps = sem("pt_ps")
        alb_ready = sem("alb_ready")
        pt_ready = sem("pt_ready")
        p_mm = sem("p_mm")
        x2s = sem("x2s")
        x2h_ready = sem("x2h_ready")
        x2l_ready = sem("x2l_ready")
        wn_ready = sem("wn_ready")
        v_ps = sem("v_ps")
        vh_ready = sem("vh_ready")
        vl_ready = sem("vl_ready")
        bz_ps = sem("bz_ps")
        bz_ready = sem("bz_ready")
        wt_ps = sem("wt_ps")
        wth_ready = sem("wth_ready")
        wtl_ready = sem("wtl_ready")
        wuh_ready = sem("wuh_ready")
        wul_ready = sem("wul_ready")
        row_sum_ready = sem("row_sum_ready")
        bias_h = sem("bias_h")
        bias_ready = sem("bias_ready")
        g_ready = sem("g_ready")
        z_ps = sem("z_ps")
        zf_ready = sem("zf_ready")
        zl_ready = sem("zl_ready")
        y_ps = sem("y_ps")
        x3_ready = sem("x3_ready")
        u_ps = sem("u_ps")
        y_free = sem("y_free")
        ve_ready = sem("ve_ready")
        rstd_ready = sem("rstd_ready")
        fin_done = sem("fin_done")
        dve_front = sem("dve_front")
        dve_back = sem("dve_back")
        dve_setup = sem("dve_setup")
        pool_own = sem("pool_own")
        x_loaded = [sem("x_loaded0"), sem("x_loaded1")]
        stored = [sem(f"stored{i}") for i in range(OB)]

        CREDIT = NJ
        CONST_DMAS, CONST_MADE = 7, 4

        X_DMAS = [6] + [3] * (NC - 2) + [6]

        def x_count(n, c):
            return n * 16 * sum(X_DMAS[c % 2::2]) + 16 * sum(X_DMAS[c % 2:c + 1:2])

        def before(t, ring):
            return t - ring if t >= ring else max(u for u in range(NJ) if u % ring == t % ring) - NJ

        def half(h):
            return slice(h * HALF, (h + 1) * HALF)

        def blk(j):
            return slice(j * P, (j + 1) * P)

        block = ctx.enter_context(nc.Block())

        @block.sync
        def _(sp):
            def col(a):
                return a.rearrange("(p o) -> p o", o=1)

            def spread(a):
                return a.rearrange("(o b) -> o b", o=1).to_broadcast([P, B])

            def load_constants():
                sp.dma_start(w1[:, :, :], L1_W1.rearrange("(k p) a -> p k a", p=P)).then_inc(const_in, 16)
                sp.dma_start(b1_col[:, :], col(L1_b1)).then_inc(const_in, 16)
                sp.dma_start(v_col[:, :], col(L1_v)).then_inc(const_in, 16)
                for q, z in enumerate((condB_zX, condB_zY, condB_zR)):
                    sp.dma_start(raw3[:, q, :], spread(z)).then_inc(const_in, 16)
                sp.dma_start(tok_i[:, :], spread(itok_B_0_2)).then_inc(const_in, 16)

            def load_x(n, c):
                sl, r0, size = c % 2, c * 2 * P, 2 * P
                wait_past(sp, l0_done, NC * n + c - 1)

                def get(dst, lo, hi):
                    src = x[bass.ds(n, 1), lo:hi, :]
                    if hi - lo == size:
                        src = src.rearrange("b (j p) d -> p (b j) d", p=P)
                    else:
                        src = src.rearrange("b p d -> p (b d)")
                    sp.dma_start(dst, src).then_inc(x_loaded[sl], 16)

                get(xn[:, sl, :, 1:D + 1], r0, r0 + size)
                if c == 0:
                    get(xu[1:113, sl, 0, :], 0, 112)
                    get(xu[113:P, sl, 0, :], 112, P - 1)
                    get(xu[0:1, sl, 0, :], 1, 2)
                    get(xu[:, sl, 1, :], P - 1, 2 * P - 1)
                    get(xd[:, sl, :, :], r0 + 1, r0 + 1 + size)
                elif c == NC - 1:
                    get(xu[:, sl, :, :], r0 - 1, r0 - 1 + size)
                    get(xd[:, sl, 0, :], r0 + 1, r0 + 1 + P)
                    get(xd[0:112, sl, 1, :], r0 + P + 1, r0 + P + 113)
                    get(xd[112:P - 1, sl, 1, :], r0 + P + 113, S)
                    get(xd[P - 1:P, sl, 1, :], S - 2, S - 1)
                else:
                    get(xu[:, sl, :, :], r0 - 1, r0 - 1 + size)
                    get(xd[:, sl, :, :], r0 + 1, r0 + 1 + size)

            def token(tok, n, count):
                return sp.value_load(tok.rearrange("(o b) -> o b", o=1)[:, bass.ds(n, 1)],
                                     min_val=0, max_val=count - 1)

            def load_weights(n):
                subject = token(itok_B_0_7, n, NSUB)
                profile = token(itok_B_0_6, n, NPROF)
                wait_past(sp, wt_ps, 2 * n)
                wait_past(sp, bz_ps, n)
                sp.dma_start(wn[:, :, :], L2_w[bass.ds(subject, 1), :, :].rearrange(
                    "s (k p) h -> p (s k) h", p=P)).then_inc(wt_loaded, 16)
                sp.dma_start(wd[:, :, :], L3_dw[bass.ds(profile, 1), :, :].rearrange(
                    "s (k p) h -> p (s k) h", p=P)).then_inc(wt_loaded, 16)
                sp.dma_start(b_col[:, :], L2_b[bass.ds(subject, 1), :].rearrange(
                    "s (k p) -> p (s k)", p=P), allow_slow_non_contiguous=True).then_inc(wt_loaded, 16)
                wait_past(sp, bz_ready, n)
                sp.dma_start(bd_col[:, :], L3_db[bass.ds(profile, 1), :].rearrange("s p -> p s")
                             ).then_inc(wt_loaded, 16)
                wait_past(sp, row_sum_ready, 2 * n)
                for q, (a, i) in enumerate(((L2_b, subject), (L3_b, profile), (L3_ub, profile))):
                    sp.dma_start(rows[:, q, :], a[bass.ds(i, 1), :].to_broadcast([P, D])
                                 ).then_inc(row_loaded, 16)
                wait_past(sp, wul_ready, n)
                wait_past(sp, g_ready, n)
                sp.dma_start(wu[:, :], L3_uw[bass.ds(profile, 1), :, :].rearrange("s p h -> p (s h)")
                             ).then_inc(up_loaded, 16)
                sp.dma_start(g_in[:, :], L3_g[bass.ds(profile, 1), :].to_broadcast([P, D])
                             ).then_inc(up_loaded, 16)

            def front(n):
                load_x(n, 0)
                load_x(n, 1)
                load_weights(n)
                load_x(n, 2)
                load_x(n, 3)

            load_constants()
            front(0)
            with sp.Fori(1, B) as n:
                front(n)

        @block.gpsimd
        def _(pool):
            own = [0]

            def link(ins):
                own[0] += 1
                ins.then_inc(pool_own, 1)
                pool.wait_ge(pool_own, own[0])

            def constants():
                link(pool.memset(ident[:, :], 0.0))
                pool.affine_select(out=ident[:, :], in_=ident[:, :], compare_op=ALU.not_equal, fill=1.0,
                                   base=0, pattern=[[-1, P]], channel_multiplier=1).then_inc(const_made, 1)
                link(pool.memset(masks[:, :, :], 0.0))
                for kind, (op, sign) in enumerate(((ALU.is_ge, 1), (ALU.is_ge, -1), (ALU.not_equal, 1))):
                    own_block = masks[:, kind, 0:P]
                    link(pool.affine_select(out=own_block, in_=own_block, compare_op=op, fill=BIG,
                                            base=0, pattern=[[-sign, P]], channel_multiplier=sign))
                for kind, (op, sign) in enumerate(((ALU.is_gt, 1), (ALU.is_gt, -1), (ALU.not_equal, 1))):
                    pairs = masks[:, kind, P:P + NB].rearrange("p (a b) -> p a b", b=NJ)
                    link(pool.affine_select(out=pairs, in_=pairs, compare_op=op, fill=BIG, base=0,
                                            pattern=[[sign, NJ], [-sign, NJ]], channel_multiplier=0))
                count = [masks[:, kind, P + NB:MASK] for kind in range(3)]
                link(pool.iota(iota_i[:, :], pattern=[[P, NJ]], base=1, channel_multiplier=1))
                link(pool.tensor_copy(count[0], iota_i[:, :]))
                link(pool.tensor_scalar(count[1], count[0], -1.0, float(S + 1), ALU.mult, ALU.add))
                pool.memset(count[2], float(S - 1)).then_inc(const_made, 1)
                link(pool.memset(ones[:, :], 1.0))
                link(pool.memset(minus_half[:, :], -0.5))
                link(pool.memset(bias_rows_f[:, :], 0.0))
                link(pool.memset(bias_rows_f[0:1, :], 1.0))
                link(pool.memset(bias_rows_f[64:65, :], 1.0))
                pool.wait_ge(const_in, 16 * CONST_DMAS)
                pool.tensor_scalar(v_rep[:, :], ones[:, :], v_col[:, 0:1], 0.0, ALU.mult,
                                   ALU.add).then_inc(const_made, 2)

            def neighbours(n, c):
                sl = c % 2
                pool.wait_ge(x_loaded[sl], x_count(n, c))
                pool.tensor_tensor(xu[:, sl, :, :], xu[:, sl, :, :], xd[:, sl, :, :],
                                   ALU.add).then_inc(pool_b, 1)
                pool.wait_ge(halo, NC * n + c + 1)
                pool.wait_ge(pool_b, NC * n + c + 1)
                pool.tensor_tensor(xd[:, sl, :, :], xn[:, sl, :, 0:D], xn[:, sl, :, 2:D + 2],
                                   ALU.add).then_inc(pool_a, 1)

            def sum_rows(n):
                pool.wait_ge(row_loaded, 48 * n + 48)
                wait_past(pool, bias_ready, n)
                pool.tensor_tensor(row_sum[:, 0, :], rows[:, 0, :], rows[:, 1, :],
                                   ALU.add).then_inc(row_sum_ready, 1)
                pool.tensor_tensor(row_sum[:, 1, :], rows[:, 2, :], rows[:, 1, :],
                                   ALU.subtract).then_inc(row_sum_ready, 1)

            def bias_rest(n):
                wait_past(pool, rstd_ready, NJ * n)
                pool.wait_ge(row_sum_ready, 2 * n + 2)
                pool.wait_ge(bias_h, n + 1)
                rest = bias[64:P, :, :]
                pool.tensor_tensor(rest, row_sum[64:P, :, :], rest.bitcast(F32),
                                   ALU.subtract).then_inc(bias_ready, 1)
                pool.wait_ge(bias_ready, n + 1)

            def root(b, t):
                r = t % TB
                pool.wait_ge(ve_ready, NJ * b + t + 1)
                pool.tensor_tensor(rstd[:, r:r + 1], ve[:, r:r + 1], minus_half[:, :],
                                   ALU.pow).then_inc(rstd_ready, 1)

            def program(b, n):
                for t in range(NJ):
                    if n is not None and t < NC:
                        neighbours(n, t)
                    if n is not None and t == 5:
                        sum_rows(n)
                    if b is not None and t >= 1:
                        root(b, t - 1)
                if b is not None:
                    root(b, NJ - 1)
                if n is not None:
                    bias_rest(n)

            constants()
            program(None, 0)
            with pool.Fori(0, B - 1) as i:
                program(i, i + 1)
            program(B - 1, None)

        @block.tensor
        def _(pe):
            mm = pe.matmul

            def split_product(dst, parts, first, last):
                for q, (lhs, rhs) in enumerate(parts):
                    ins = mm(dst, lhs, rhs, start=first and q == 0, stop=last and q == len(parts) - 1,
                             skip_group_check=True)
                return ins

            def transpose_x1(n, c):
                pe.wait_ge(l0_done, NC * n + c + 1)
                wait_past(pe, *((zf_ready, 4 * n), (x2s, KD * n), (x1t_ready, NC * n + 1),
                                (x1t_ready, NC * n + 2))[c])
                pair = (pair_a, pair_b)[c % 2]
                for k in range(KD):
                    for j in range(2):
                        ins = pe.transpose(pair[:, k * 2 * P + j * P:k * 2 * P + (j + 1) * P],
                                           x1[:, 2 * c + j, blk(k)], ident[:, :])
                ins.then_inc(xt_ps, 1)

            def score_hidden(n):
                pe.wait_ge(x1t_ready, NC * n + NC)
                for h in range(2):
                    for k in range(KD):
                        ins = mm(pair_a[:, half(h)], w1[:, k, :], x1t[:, k, half(h)],
                                 start=k == 0, stop=k == KD - 1)
                    ins.then_inc(h_ps, 1)

            def scores(n):
                for h in range(2):
                    pe.wait_ge(th_ready, 2 * n + h + 1)
                    mm(pair_b[:, half(h)], v_rep[:, :], th[:, half(h)], start=True, stop=True
                       ).then_inc(sc_ps, 1)
                wait_past(pe, bz_ready, n)
                for j in range(NJ):
                    ins = mm(SN[:, j:j + 1], th[:, blk(j)], v_col[:, :], start=True, stop=True)
                ins.then_inc(sn_ps, 1)

            def down_through_w(n):
                pe.wait_ge(wn_ready, n + 1)
                pe.wait_ge(th_ready, 2 * n + 2)
                for hb in range(KD):
                    for ob in range(KD):
                        ins = mm(pair_a[:, blk(hb)], wn[:, ob, blk(hb)], wd[:, ob, :],
                                 start=ob == 0, stop=ob == KD - 1)
                ins.then_inc(v_ps, 1)

            def block_sums(n):
                pe.wait_ge(ex_ready, n + 1)
                mm(cbank[:, ZG:ZG + NJ], ones[:, :], E_ROW, start=True, stop=True)
                for k in range(KD):
                    for j in range(NJ):
                        o = ZG + (k + 1) * NJ + j
                        ins = mm(cbank[:, o:o + 1], x1[:, j, blk(k)], E_ROW[:, j:j + 1],
                                 start=True, stop=True)
                ins.then_inc(g_ps, 1)

            def adapter_bias(n):
                pe.wait_ge(cc_ready, n + 1)
                for ob in range(KD):
                    ins = mm(cbank[:, BZ:BZ + 1], wd[:, ob, :], b_col[:, ob:ob + 1],
                             start=ob == 0, stop=ob == KD - 1)
                ins.then_inc(bz_ps, 1)

            def transpose_w(n, q):
                pe.wait_ge(*((vl_ready, n + 1), (sb_read, n + 1))[q])
                pair = (pair_a, pair_b)[q]
                for hb in (2 * q, 2 * q + 1):
                    for ob in range(KD):
                        o = (hb % 2) * D + ob * P
                        ins = pe.transpose(pair[:, o:o + P], wn[:, ob, blk(hb)], ident[:, :])
                ins.then_inc(wt_ps, 1)

            def transpose_p(n):
                pe.wait_ge(pn_ready, n + 1)
                pe.wait_ge(wtl_ready, 2 * n + 1)
                for j in range(NJ):
                    ins = pe.transpose(pair_a[:, blk(j)], pn[:, blk(j)], ident[:, :])
                ins.then_inc(pt_ps, 1)

            def transpose_alpha(n):
                pe.wait_ge(al_ready, n + 1)
                pe.wait_ge(wtl_ready, 2 * n + 2)
                for j in range(NJ):
                    ins = pe.transpose(pair_b[:, blk(j)], AL[:, j:j + 1].to_broadcast([P, P]), ident[:, :])
                ins.then_inc(al_ps, 1)

            def pool_own_block(n, k):
                pe.wait_ge(*((pt_ready, n + 1), (alb_ready, n + 1), (x2s, KD * n + 1),
                             (x2s, KD * n + 2))[k])
                pair = (pair_a, pair_b)[k % 2]
                for j in range(NJ):
                    ins = mm(pair[:, blk(j)], x1[:, j, blk(k)], pt[:, blk(j)], start=True, stop=True)
                ins.then_inc(p_mm, 1)

            def adapter_down(n):
                pe.wait_ge(x2s, KD * n + 3)
                pe.wait_ge(vl_ready, n + 1)
                for h in range(2):
                    for k in range(KD):
                        if h == 0:
                            pe.wait_ge(x2l_ready, KD * n + k + 1)
                        ins = split_product(pair_a[:, half(h)], (
                            (vh[:, k, :], x2h[:, k, half(h)]), (vl[:, k, :], x2h[:, k, half(h)]),
                            (vh[:, k, :], x2l[:, k, half(h)])), k == 0, k == KD - 1)
                    ins.then_inc(z_ps, 1)

            def linear(b, t):
                y = ys[t % YB]
                if t == 0:
                    pe.wait_ge(bias_ready, b + 1)
                    pe.wait_ge(wtl_ready, 2 * b + 2)
                pe.wait_ge(y_free, NJ * b + before(t, YB) + 1 + CREDIT)
                mm(y[:, :], bias_rows_on[:, :], bias[:, 0, :], start=True, stop=False, skip_group_check=True)
                for k in range(KD):
                    ins = split_product(y[:, :], (
                        (x2h[:, k, blk(t)], wth[:, k, :]), (x2h[:, k, blk(t)], wtl[:, k, :]),
                        (x2l[:, k, blk(t)], wth[:, k, :])), False, k == KD - 1)
                ins.then_inc(y_ps, 1)

            def adapter_up(b, t):
                y = ys[t % YB]
                pe.wait_ge(x3_ready, NJ * b + t + 1)
                if t == 0:
                    pe.wait_ge(wul_ready, b + 1)
                if t % (NJ // 2) == 0:
                    pe.wait_ge(zl_ready, 2 * b + t // (NJ // 2) + 1)
                mm(y[:, :], bias_rows_on[:, :], bias[:, 1, :], start=False, stop=False, skip_group_check=True)
                ins = split_product(y[:, :], ((zh[:, blk(t)], wuh[:, :]), (zh[:, blk(t)], wul[:, :]),
                                              (zl[:, blk(t)], wuh[:, :])), False, True)
                ins.then_inc(u_ps, 1)

            def program(b, n):
                for t in range(NJ):
                    if b is not None:
                        linear(b, t)
                    if n is not None:
                        if 2 <= t <= 5:
                            transpose_x1(n, t - 2)
                        if t == 5:
                            score_hidden(n)
                        if t == 6:
                            scores(n)
                            down_through_w(n)
                        if t == 7:
                            block_sums(n)
                    if b is not None and t >= 1:
                        adapter_up(b, t - 1)
                if n is not None:
                    transpose_w(n, 0)
                    transpose_w(n, 1)
                    adapter_bias(n)
                if b is not None:
                    adapter_up(b, NJ - 1)
                if n is not None:
                    transpose_p(n)
                    transpose_alpha(n)
                    for k in range(KD):
                        pool_own_block(n, k)
                    adapter_down(n)

            pe.wait_ge(const_made, CONST_MADE)
            pe.wait_ge(table_made, 1)
            program(None, 0)
            with pe.Fori(0, B - 1) as i:
                program(i, i + 1)
            program(B - 1, None)

        @block.scalar
        def _(act):
            def copy(dst, src):
                return act.activation(dst, src, ACT.Identity)

            def centre(n, c):
                sl = c % 2
                act.wait_ge(x_loaded[sl], x_count(n, c))
                copy(xn[:, sl, :, 0:D + 2:D + 1], xn[:, sl, :, 2:D:D - 3]).then_inc(halo, 1)
                act.wait_ge(cur_ready, n + 1)
                wait_past(act, p_mm, KD * n)
                act.activation(x1[:, 2 * c:2 * c + 2, :], xn[:, sl, :, 1:D + 1], ACT.Identity,
                               bias=cur[:, CENTRE:CENTRE + 1], scale=cur[:, MINUS_R:MINUS_R + 1]
                               ).then_inc(c_done, 1)

            def keep_x1t(n, c):
                act.wait_ge(xt_ps, NC * n + c + 1)
                wait_past(act, h_ps, 2 * n)
                pair = (pair_a, pair_b)[c % 2]
                copy(x1t[:, :, c * 2 * P:(c + 1) * 2 * P],
                     pair[:, :].rearrange("p (k q) -> p k q", k=KD)).then_inc(x1t_ready, 1)

            def hidden(n):
                wait_past(act, sn_ps, n)
                for h in range(2):
                    act.wait_ge(h_ps, 2 * n + h + 1)
                    act.activation(th[:, half(h)], pair_a[:, half(h)], ACT.Tanh,
                                   bias=b1_col[:, 0:1]).then_inc(th_ready, 1)

            def exps(n):
                act.wait_ge(arg_ready, n + 1)
                wait_past(act, g_ps, n)
                act.activation(EX, ARG, ACT.Exp).then_inc(ex_ready, 1)
                act.wait_ge(negm_ready, n + 1)
                for j in range(NJ):
                    ins = act.activation(pn[:, blk(j)], pn[:, blk(j)], ACT.Exp, bias=NEGM[:, j:j + 1],
                                         accum_out=ZD[:, j:j + 1])
                ins.then_inc(p_exp, 1)

            def round_v(n):
                act.wait_ge(v_ps, n + 1)
                wait_past(act, z_ps, 2 * n)
                copy(vh[:, :, :], pair_a[:, 0:KD * P].rearrange("p (k q) -> p k q", k=KD)
                     ).then_inc(vh_ready, 1)

            def round_w(n, q):
                act.wait_ge(wt_ps, 2 * n + q + 1)
                wait_past(act, y_ps, NJ * n)
                copy(wth[:, 2 * q:2 * q + 2, :], (pair_a, pair_b)[q][:, :].rearrange(
                    "p (k q) -> p k q", k=2)).then_inc(wth_ready, 1)

            def round_up(n):
                act.wait_ge(up_loaded, 32 * n + 32)
                wait_past(act, u_ps, NJ * n)
                copy(wuh[:, :], wu[:, :]).then_inc(wuh_ready, 1)
                act.wait_ge(row_sum_ready, 2 * n + 2)
                copy(bias[:, :, :], row_sum[:, :, :]).then_inc(bias_h, 1)

            def keep_p(n):
                act.wait_ge(pt_ps, n + 1)
                wait_past(act, p_mm, KD * n)
                copy(pt[:, :], pair_a[:, :]).then_inc(pt_ready, 1)
                act.wait_ge(al_ps, n + 1)
                wait_past(act, x2s, KD * n)
                copy(alb[:, :], pair_b[:, :]).then_inc(alb_ready, 1)

            def round_x2(n, k):
                act.wait_ge(x2s, KD * n + k + 1)
                copy(x2h[:, k, :], x2f[:, k % 2, :]).then_inc(x2h_ready, 1)

            def adapter_relu(n):
                act.wait_ge(bz_ready, n + 1)
                for h in range(2):
                    act.wait_ge(z_ps, 2 * n + h + 1)
                    act.activation(zf[:, half(h)], pair_a[:, half(h)], ACT.Relu,
                                   bias=bz[:, 0:1]).then_inc(zf_ready, 1)
                    act.activation(zh[:, half(h)], pair_a[:, half(h)], ACT.Relu,
                                   bias=bz[:, 0:1]).then_inc(zf_ready, 1)

            def keep_x3(b, t):
                act.wait_ge(y_ps, NJ * b + t + 1)
                act.wait_ge(fin_done, NJ * b + before(t, XB) + 1 + CREDIT)
                copy(x3[:, t % XB, :], ys[t % YB][:, :]).then_inc(x3_ready, 1)

            def store(b, t):
                act.wait_ge(fin_done, NJ * b + t + 1 + CREDIT)
                act.dma_start(out[bass.ds(b, 1), blk(t), :].rearrange("b p d -> p (b d)"),
                              o_sb[:, t % OB, :]).then_inc(stored[t % OB], 16)

            def program(b, n):
                for t in range(NJ):
                    if n is not None and t < NC:
                        centre(n, t)
                    if b is not None:
                        keep_x3(b, t)
                        if t >= 3:
                            store(b, t - 3)
                    if n is not None:
                        if 2 <= t <= 5:
                            keep_x1t(n, t - 2)
                        if t == 5:
                            hidden(n)
                        if t == 6:
                            round_v(n)
                            exps(n)
                if n is not None:
                    round_w(n, 0)
                    round_w(n, 1)
                if b is not None:
                    store(b, NJ - 3)
                if n is not None:
                    keep_p(n)
                    round_up(n)
                if b is not None:
                    store(b, NJ - 2)
                    store(b, NJ - 1)
                if n is not None:
                    for k in range(KD):
                        round_x2(n, k)
                    adapter_relu(n)

            act.wait_ge(const_in, 16 * CONST_DMAS)
            program(None, 0)
            with act.Fori(0, B - 1) as i:
                program(i, i + 1)
            program(B - 1, None)
            for q in range(OB):
                act.wait_ge(stored[q], 16 * (B * NJ // OB) + 16)

        @block.vector
        def _(dve):
            front = Chain(dve_front, 16 + NC * 2)
            back = Chain(dve_back, 2 * NJ)

            def by_j(a):
                return a.rearrange("p (a b) -> p a b", b=NJ)

            def make_table():
                made = [0]

                def link(ins):
                    made[0] += 1
                    ins.then_inc(dve_setup, 1)
                    dve.wait_ge(dve_setup, made[0])

                dve.wait_ge(const_in, 16 * CONST_DMAS)
                zx, zy, zr = (raw3[:, q, :] for q in range(3))
                link(dve.tensor_copy(tok_f[:, :], tok_i[:, :]))
                link(dve.tensor_copy(table[:, Z_X:Z_Y + 1, :], raw3[:, 0:2, :]))
                link(dve.tensor_scalar(table[:, MINUS_R, :], zr, -1.0, None, ALU.mult))
                link(dve.tensor_scalar(table[:, IS_PREFIX, :], tok_f[:, :], 0.0, None, ALU.is_equal))
                link(dve.tensor_scalar(table[:, IS_POSTFIX, :], tok_f[:, :], 1.0, None, ALU.is_equal))
                centre, cloze = table[:, CENTRE, :], table[:, IS_CLOZE, :]
                link(dve.tensor_scalar(centre, zx, -2.0, 1.0, ALU.mult, ALU.add))
                link(dve.scalar_tensor_tensor(out=centre, in0=zy, scalar=-2.0, in1=centre,
                                              op0=ALU.mult, op1=ALU.add))
                link(dve.tensor_tensor(centre, centre, zr, ALU.add))
                link(dve.tensor_scalar(cloze, table[:, IS_PREFIX, :], -1.0, 1.0, ALU.mult, ALU.add))
                link(dve.tensor_tensor(cloze, cloze, table[:, IS_POSTFIX, :], ALU.subtract))
                dve.wait_ge(const_made, CONST_MADE)
                dve.tensor_copy(bias_rows_on[:, :], bias_rows_f[:, :]).then_inc(table_made, 1)

            def take_scalars(n):
                front.start(n)
                wait_past(dve, c_done, NC * n)
                dve.tensor_copy(cur[:, :], table[:, :, bass.ds(n, 1)].rearrange("p a b -> p (a b)")
                                ).then_inc(cur_ready, 1)
                dve.wait_ge(cur_ready, n + 1)
                front.mark(dve.tensor_scalar(mask[:, :], masks[:, 2, :], cur[:, IS_CLOZE:IS_CLOZE + 1],
                                             None, ALU.mult))
                for kind, col in ((1, IS_POSTFIX), (0, IS_PREFIX)):
                    front.wait(dve)
                    front.mark(dve.scalar_tensor_tensor(
                        out=mask[:, :], in0=masks[:, kind, :], scalar=cur[:, col:col + 1],
                        in1=mask[:, :], op0=ALU.mult, op1=ALU.add))

            def diffuse(n, c):
                sl = c % 2
                o = x1[:, 2 * c:2 * c + 2, :]
                dve.wait_ge(c_done, NC * n + c + 1)
                front.mark(dve.tensor_tensor(o, o, xn[:, sl, :, 1:D + 1], ALU.mult))
                dve.wait_ge(pool_a, NC * n + c + 1)
                dve.wait_ge(pool_b, NC * n + c + 1)
                front.wait(dve)
                front.mark(dve.scalar_tensor_tensor(out=o, in0=xd[:, sl, :, :], scalar=cur[:, Z_X:Z_X + 1],
                                                    in1=o, op0=ALU.mult, op1=ALU.add))
                front.wait(dve)
                dve.scalar_tensor_tensor(out=o, in0=xu[:, sl, :, :], scalar=cur[:, Z_Y:Z_Y + 1],
                                         in1=o, op0=ALU.mult, op1=ALU.add).then_inc(l0_done, 1)

            def add_identity(n):
                dve.wait_ge(wt_loaded, 64 * n + 64)
                diagonal = wn[:, :, :].rearrange("p k h -> p (k h)")
                for k in range(KD):
                    d = diagonal[:, k * (D + P):k * (D + P) + P]
                    ins = dve.tensor_tensor(d, d, ident[:, :], ALU.add)
                ins.then_inc(wn_ready, 1)

            def maxima(n):
                wait_past(dve, pt_ps, n)
                own_mask = mask[:, 0:P].rearrange("p (o l) -> p o l", o=1).to_broadcast([P, NJ // 2, P])
                for h in range(2):
                    dve.wait_ge(sc_ps, 2 * n + h + 1)
                    front.mark(dve.tensor_tensor(pn[:, half(h)].rearrange("p (j l) -> p j l", l=P),
                                                 pair_b[:, half(h)].rearrange("p (j l) -> p j l", l=P),
                                                 own_mask, ALU.add))
                for h in range(2):
                    ins = dve.tensor_reduce(MI[:, 4 * h:4 * h + 4],
                                            pair_b[:, half(h)].rearrange("p (j l) -> p j l", l=P),
                                            AX.X, ALU.max)
                ins.then_inc(sb_read, 1)
                front.wait(dve)
                front.mark(dve.tensor_reduce(MDIAG, pn[:, :].rearrange("p (j l) -> p j l", l=P),
                                             AX.X, ALU.max))
                dve.wait_ge(sb_read, n + 1)
                mi_all = MI.rearrange("p (o i) -> p o i", o=1).to_broadcast([P, NJ, NJ])
                front.mark(dve.tensor_tensor(by_j(KM), by_j(mask[:, P:P + NB]), mi_all, ALU.add))
                front.wait(dve)
                front.mark(dve.tensor_reduce(MCAR, by_j(KM), AX.X, ALU.max))
                front.wait(dve)
                front.mark(dve.tensor_tensor(M, MDIAG, MCAR, ALU.max))
                front.wait(dve)
                wait_past(dve, p_exp, n)
                dve.tensor_scalar(NEGM, M, -1.0, None, ALU.mult).then_inc(negm_ready, 1)
                dve.wait_ge(sn_ps, n + 1)
                front.mark(dve.tensor_tensor(ARG[:, 0:NJ], SN, MI, ALU.subtract))
                mcar_all = MCAR.rearrange("p (j o) -> p j o", o=1).to_broadcast([P, NJ, NJ])
                front.mark(dve.tensor_tensor(by_j(ARG[:, NJ:NJ + NB]), by_j(KM), mcar_all, ALU.subtract))
                dve.tensor_tensor(ARG[:, NJ + NB:], MCAR, M, ALU.subtract).then_inc(arg_ready, 1)

            def rest_v(n):
                dve.wait_ge(vh_ready, n + 1)
                dve.tensor_tensor(vl[:, :, :], pair_a[:, 0:KD * P].rearrange("p (k q) -> p k q", k=KD),
                                  vh[:, :, :].bitcast(F32), ALU.subtract).then_inc(vl_ready, 1)

            def probabilities(n):
                dve.wait_ge(g_ps, n + 1)
                dve.wait_ge(ex_ready, n + 1)
                kap = by_j(KAP).rearrange("p (o a) b -> p o (a b)", o=1).to_broadcast([P, KD + 1, NB])
                sums = cbank[:, ZG:ZG + (KD + 1) * NJ].rearrange("p (k o i) -> p k o i", k=KD + 1, o=1
                                                                ).to_broadcast([P, KD + 1, NJ, NJ])
                front.mark(dve.tensor_tensor(prod[:, :, :, :], sums,
                                             kap.rearrange("p k (a b) -> p k a b", b=NJ), ALU.mult))
                front.wait(dve)
                dve.tensor_reduce(CC, prod[:, :, :, :].rearrange("p k a b -> p (k a) b"),
                                  AX.X, ALU.add).then_inc(cc_ready, 1)
                dve.wait_ge(cc_ready, n + 1)
                front.mark(dve.tensor_tensor(ZT, ALH, CC[:, 0:NJ], ALU.mult))
                dve.wait_ge(p_exp, n + 1)
                front.wait(dve)
                front.mark(dve.tensor_tensor(ZT2, ZT, ZD, ALU.add))
                front.wait(dve)
                front.mark(dve.tensor_tensor(ZT, ZT2, mask[:, P + NB:MASK], ALU.mult))
                front.wait(dve)
                front.mark(dve.reciprocal(RZ, ZT))
                front.wait(dve)
                wait_past(dve, al_ps, n)
                dve.tensor_tensor(AL, ALH, RZ, ALU.mult).then_inc(al_ready, 1)
                for j in range(NJ):
                    ins = dve.scalar_tensor_tensor(out=pn[:, blk(j)], in0=pn[:, blk(j)],
                                                   scalar=RZ[:, j:j + 1], in1=ident[:, :],
                                                   op0=ALU.mult, op1=ALU.add)
                ins.then_inc(pn_ready, 1)

            def adapter_bias(n):
                dve.wait_ge(bz_ps, n + 1)
                wait_past(dve, zf_ready, 4 * n)
                dve.tensor_tensor(bz[:, :], cbank[:, BZ:BZ + 1], bd_col[:, :], ALU.add).then_inc(bz_ready, 1)

            def rest_w(n, q):
                dve.wait_ge(wth_ready, 2 * n + q + 1)
                dve.tensor_tensor(wtl[:, 2 * q:2 * q + 2, :], (pair_a, pair_b)[q][:, :].rearrange(
                    "p (k q) -> p k q", k=2), wth[:, 2 * q:2 * q + 2, :].bitcast(F32),
                    ALU.subtract).then_inc(wtl_ready, 1)

            def rest_up(n):
                dve.wait_ge(wuh_ready, n + 1)
                dve.tensor_tensor(wul[:, :], wu[:, :], wuh[:, :].bitcast(F32),
                                  ALU.subtract).then_inc(wul_ready, 1)
                dve.wait_ge(up_loaded, 32 * n + 32)
                dve.tensor_copy(g_row[:, :], g_in[:, :]).then_inc(g_ready, 1)

            def add_carry(n, k):
                dve.wait_ge(p_mm, KD * n + k + 1)
                dve.wait_ge(alb_ready, n + 1)
                wait_past(dve, x2h_ready, KD * n + k - 1)
                wait_past(dve, x2l_ready, KD * n + k - 1)
                pair = (pair_a, pair_b)[k % 2]
                for j in range(NJ):
                    o = (k + 1) * NJ + j
                    ins = dve.scalar_tensor_tensor(out=x2f[:, k % 2, blk(j)], in0=alb[:, blk(j)],
                                                   scalar=CC[:, o:o + 1], in1=pair[:, blk(j)],
                                                   op0=ALU.mult, op1=ALU.add)
                ins.then_inc(x2s, 1)

            def rest_x2(n, k):
                dve.wait_ge(x2h_ready, KD * n + k + 1)
                dve.tensor_tensor(x2l[:, k, :], x2f[:, k % 2, :], x2h[:, k, :].bitcast(F32),
                                  ALU.subtract).then_inc(x2l_ready, 1)

            def rest_z(n):
                for h in range(2):
                    dve.wait_ge(zf_ready, 4 * n + 2 * h + 2)
                    dve.tensor_tensor(zl[:, half(h)], zf[:, half(h)], zh[:, half(h)].bitcast(F32),
                                      ALU.subtract).then_inc(zl_ready, 1)

            def normalise(b, t):
                y, r = ys[t % YB], t % TB
                if t == 0:
                    back.start(b)
                dve.wait_ge(u_ps, NJ * b + t + 1)
                back.mark(dve.bn_stats(stats[:, r, :], y[:, :]))
                if t == 0:
                    back.wait(dve)
                    dve.memset(carrier[:, :], 0.0)
                else:
                    finish(b, t - 1)
                back.mark(dve.bn_aggr(mv[:, r, :], stats[:, r, :]))
                back.wait(dve)
                dve.tensor_scalar(ve[:, r:r + 1], mv[:, r, 1:2], EPS, None, ALU.add).then_inc(ve_ready, 1)
                dve.wait_ge(g_ready, b + 1)
                dve.scalar_tensor_tensor(out=t1[:, r, :], in0=y[:, :], scalar=mv[:, r, 0:1], in1=g_row[:, :],
                                         op0=ALU.subtract, op1=ALU.mult).then_inc(y_free, 1)

            def finish(b, t):
                r = t % TB
                dve.wait_ge(rstd_ready, NJ * b + t + 1)
                dve.wait_ge(y_free, NJ * b + t + 1 + CREDIT)
                dve.wait_ge(x3_ready, NJ * b + t + 1)
                dve.wait_ge(stored[t % OB], 16 * (2 * b + t // OB) + 16)
                back.wait(dve)
                dve.scalar_tensor_tensor(out=o_sb[:, t % OB, :], in0=t1[:, r, :], scalar=rstd[:, r:r + 1],
                                         in1=x3[:, t % XB, :], op0=ALU.mult, op1=ALU.add
                                         ).then_inc(fin_done, 1)

            def program(b, n):
                for t in range(NJ):
                    if n is not None:
                        if t == 0:
                            take_scalars(n)
                        if t < NC:
                            diffuse(n, t)
                        if t == 5:
                            add_identity(n)
                        if t == 6:
                            maxima(n)
                            rest_v(n)
                    if b is not None and t >= 1:
                        normalise(b, t - 1)
                if n is not None:
                    probabilities(n)
                    rest_w(n, 0)
                    rest_w(n, 1)
                    adapter_bias(n)
                if b is not None:
                    normalise(b, NJ - 1)
                    finish(b, NJ - 1)
                if n is not None:
                    rest_up(n)
                    add_carry(n, 0)
                    for k in range(1, KD):
                        add_carry(n, k)
                        rest_x2(n, k - 1)
                    rest_x2(n, KD - 1)
                    rest_z(n)
                    front.end()

            dve.sem_inc(y_free, CREDIT)
            dve.sem_inc(fin_done, CREDIT)
            for q in range(OB):
                dve.sem_inc(stored[q], 16)
            make_table()
            program(None, 0)
            with dve.Fori(0, B - 1) as i:
                program(i, i + 1)
            program(B - 1, None)


_INS = ["x", "condB_zX", "condB_zY", "condB_zR", "itok_B_0_2", "itok_B_0_7", "itok_B_0_6",
        "L1_cond_W1", "L1_cond_b1", "L1_cond_v", "L2_cond_weight", "L2_cond_bias", "L3_cond_down_w",
        "L3_cond_down_b", "L3_cond_up_w", "L3_cond_up_b", "L3_cond_ln_g", "L3_cond_ln_b"]


def kernel(**inputs):
    import concourse.bacc as bacc
    from concourse.bass_utils import run_bass_kernel_spmd

    nc = bacc.Bacc("TRN2", target_bir_lowering=False, num_devices=1)
    arrays, args = {}, []
    for name in _INS:
        a = np.ascontiguousarray(inputs[name])
        arrays[f"in_{name}"] = a
        args.append(nc.dram_tensor(f"in_{name}", a.shape, mybir.dt.from_np(a.dtype),
                                   kind="ExternalInput").ap())
    out = nc.dram_tensor("out_0", inputs["x"].shape, F32, kind="ExternalOutput").ap()
    build(nc, *args, out)
    return run_bass_kernel_spmd(nc, [arrays], core_ids=[0]).results[0]["out_0"]
```

```python
from contextlib import ExitStack

import numpy as np
import concourse.bass as bass
from concourse import mybir

F32 = mybir.dt.float32
F32R = mybir.dt.float32r
I32 = mybir.dt.int32
ALU = mybir.AluOpType
ACT = mybir.ActivationFunctionType
AX = mybir.AxisListType

P = 128
BIG = -1.0e30
EPS = 1e-5
TABLE = 7
Z_X, Z_Y, CENTRE, MINUS_R, IS_PREFIX, IS_POSTFIX, IS_CLOZE = range(7)


def wait_past(eng, sem, count):
    if isinstance(count, int) and count <= 0:
        return
    eng.wait_ge(sem, count)


class Chain:

    def __init__(self, sem, per_batch):
        self.sem, self.per_batch, self.n, self.base = sem, per_batch, 0, 0

    def start(self, batch):
        self.n, self.base = 0, batch * self.per_batch

    def mark(self, ins):
        ins.then_inc(self.sem, 1)
        self.n += 1
        return self.n

    def wait(self, eng, n=None):
        eng.wait_ge(self.sem, self.base + (self.n if n is None else n))

    def end(self):
        assert self.n == self.per_batch, (self.n, self.per_batch)


def build(nc, x, condB_zX, condB_zY, condB_zR, itok_B_0_2, itok_B_0_7, itok_B_0_6,
          L1_W1, L1_b1, L1_v, L2_w, L2_b, L3_dw, L3_db, L3_uw, L3_ub, L3_g, L3_b, out):
    B, S, D = x.shape
    A = L1_W1.shape[1]
    NJ = S // P
    KD = D // P
    NC = NJ // 2
    NSUB, NPROF = L2_w.shape[0], L3_dw.shape[0]
    assert A == P and NJ == 8 and KD == 4
    HALF = S // 2
    NB = NJ * NJ
    MASK = P + NB + NJ
    YB, XB, OB = 3, 3, 4

    with ExitStack() as ctx:
        def sb(name, shape, dt=F32):
            return ctx.enter_context(nc.sbuf_tensor(name, shape, dt))

        def ps(name, cols):
            return ctx.enter_context(nc.psum_tensor(name, [P, cols], F32))

        def sem(name):
            return ctx.enter_context(nc.semaphore(name))

        ident = sb("ident", [P, P])
        masks = sb("masks", [P, 3, MASK])
        rows_on = sb("rows_on", [P, 2, P], F32R)
        ones = sb("ones", [P, P])
        v_rep = sb("v_rep", [P, P])
        v_col = sb("v_col", [P, 1])
        b1_col = sb("b1_col", [P, 1])
        w1 = sb("w1", [P, KD, A])
        raw3 = sb("raw3", [P, 3, B])
        iota_i = sb("iota_i", [P, NJ], I32)
        tok_i = sb("tok_i", [P, B], I32)
        tok_f = sb("tok_f", [P, B])
        table = sb("table", [P, TABLE, B])
        xn = sb("xn", [P, 2, 2, D + 2])
        xu = sb("xu", [P, 2, 2, D])
        xd = sb("xd", [P, 2, 2, D])
        x1 = sb("x1", [P, NJ, D])
        cur = sb("cur", [P, TABLE])
        mask = sb("mask", [P, MASK])
        pn = sb("pn", [P, S])
        th_pt = sb("th_pt", [P, NJ, P + 1])
        th, pt = th_pt[:, :, :].rearrange("p j l -> p (j l)")[:, 0:S], th_pt
        alb = sb("alb", [P, S])
        rows_on_f = pn[:, 0:2 * P].rearrange("p (i m) -> p i m", i=2)
        small = sb("small", [P, 3 * P])
        prod = sb("prod", [P, 2, NJ, NJ])
        x2f = sb("x2f", [P, 2, S])
        x1t, x2h, x2l = [], [], []
        for q in range(2):
            with nc.sbuf_tensor(f"x1t{q}", [P, KD, S], F32) as a:
                x1t.append(a)
            x2l.append(sb(f"x2l{q}", [P, KD, S], F32R))
            x2h.append(sb(f"x2h{q}", [P, KD, S], F32R))
        wn = sb("wn", [P, KD, D])
        wth = sb("wth", [P, KD, D], F32R)
        wtl = sb("wtl", [P, KD, D], F32R)
        wd = sb("wd", [P, KD, P])
        vh = sb("vh", [P, KD, P], F32R)
        vl = sb("vl", [P, KD, P], F32R)
        wu = sb("wu", [P, D])
        wuh = sb("wuh", [P, 2, D], F32R)
        wul = sb("wul", [P, 2, D], F32R)
        b_col = sb("b_col", [P, KD])
        bd_col = sb("bd_col", [P, 1])
        bz = sb("bz", [P, 1])
        rows = sb("rows", [P, D])
        bias = sb("bias", [P, 2, D], F32R)
        g_row = sb("g_row", [P, 2, D])
        zf = x2f[:, 0, :]
        zh = sb("zh", [P, S], F32R)
        zl = sb("zl", [P, S], F32R)
        x3 = sb("x3", [P, XB, D])
        o_sb = sb("o_sb", [P, OB, D])
        stats = sb("stats", [P, OB, 6])
        mv = sb("mv", [P, OB, 2])
        ve = sb("ve", [P, OB])
        minus_half = sb("minus_half", [P, 1])
        rstd = sb("rstd", [P, OB])
        carrier = sb("carrier", [P, 1])

        ys = [ps(f"y{i}", D) for i in range(YB)]
        NF = 5
        front_ps = ctx.enter_context(nc.psum_tensor("front_ps", [P, NF, 512], F32))
        pair_a = front_ps[:, 0:2, :].rearrange("p b n -> p (b n)")
        pair_b = front_ps[:, 2:4, :].rearrange("p b n -> p (b n)")
        cbank = front_ps[:, 4, :]
        hidden_ps = (cbank, pair_a[:, 0:512])
        SN, ZG = cbank[:, 0:NJ], cbank[:, NJ:2 * NJ]
        BZ = pair_a[:, 512:513]
        GROUPS = ((0, 3), (3, 6), (6, 8))
        GROUP_BANK = ((0, 1, 2), (3, 4, 2))
        NG = len(GROUPS)

        off = [0]

        def cols(n):
            off[0] += n
            return small[:, off[0] - n:off[0]]

        MI = cols(NJ)
        MDIAG, MCAR, M, NEGM = cols(NJ), cols(NJ), cols(NJ), cols(NJ)
        KM = cols(NB)
        ARG = cols(2 * NJ + NB)
        EX = cols(2 * NJ + NB)
        E_ROW, KAP, ALH = EX[:, 0:NJ], EX[:, NJ:NJ + NB], EX[:, NJ + NB:]
        ZD, CC, ZT, RZ, AL = cols(NJ), cols((KD + 1) * NJ), cols(NJ), cols(NJ), cols(NJ)
        ZT2 = cols(NJ)

        const_in = sem("const_in")
        const_made = sem("const_made")
        table_made = sem("table_made")
        cur_ready = sem("cur_ready")
        wt_loaded = sem("wt_loaded")
        row_loaded = sem("row_loaded")
        up_loaded = sem("up_loaded")
        halo = sem("halo")
        c_done = sem("c_done")
        pool_a = sem("pool_a")
        pool_b = sem("pool_b")
        l0_done = sem("l0_done")
        xt_ps = sem("xt_ps")
        x1t_ready = sem("x1t_ready")
        h_ps = sem("h_ps")
        th_ready = sem("th_ready")
        sc_ps = sem("sc_ps")
        sn_ps = sem("sn_ps")
        sb_read = sem("sb_read")
        arg_ready = sem("arg_ready")
        ex_ready = sem("ex_ready")
        negm_ready = sem("negm_ready")
        p_exp = sem("p_exp")
        g_ps = sem("g_ps")
        cc_ready = sem("cc_ready")
        al_ready = sem("al_ready")
        pn_ready = sem("pn_ready")
        al_ps = sem("al_ps")
        pt_ps = sem("pt_ps")
        alb_ready = sem("alb_ready")
        pt_ready = sem("pt_ready")
        p_mm = sem("p_mm")
        x2s = sem("x2s")
        x2h_ready = sem("x2h_ready")
        x2l_ready = sem("x2l_ready")
        wn_ready = sem("wn_ready")
        v_ps = sem("v_ps")
        vh_ready = sem("vh_ready")
        vl_ready = sem("vl_ready")
        bz_ps = sem("bz_ps")
        bz_ready = sem("bz_ready")
        wt_ps = sem("wt_ps")
        wth_ready = sem("wth_ready")
        wtl_ready = sem("wtl_ready")
        wuh_ready = sem("wuh_ready")
        wul_ready = sem("wul_ready")
        bias_h = sem("bias_h")
        bias_ready = sem("bias_ready")
        g_loaded = sem("g_loaded")
        z_ps = sem("z_ps")
        zf_ready = sem("zf_ready")
        zl_ready = sem("zl_ready")
        y_ps = sem("y_ps")
        x3_ready = sem("x3_ready")
        u_ps = sem("u_ps")
        y_free = sem("y_free")
        mv_ready = sem("mv_ready")
        ve_ready = sem("ve_ready")
        rstd_ready = sem("rstd_ready")
        scaled = sem("scaled")
        fin_done = sem("fin_done")
        dve_opening = sem("dve_opening")
        dve_front = sem("dve_front")
        dve_back = sem("dve_back")
        dve_setup = sem("dve_setup")
        pool_own = sem("pool_own")
        x_loaded = [sem("x_loaded0"), sem("x_loaded1")]
        stored = [sem(f"stored{i}") for i in range(OB)]

        CREDIT = NJ
        CONST_DMAS, CONST_MADE = 7, 4

        X_DMAS = [6] + [3] * (NC - 2) + [6]

        def x_count(n, c):
            return n * 16 * sum(X_DMAS[c % 2::2]) + 16 * sum(X_DMAS[c % 2:c + 1:2])

        def before(t, ring):
            return t - ring if t >= ring else max(u for u in range(NJ) if u % ring == t % ring) - NJ

        def half(h):
            return slice(h * HALF, (h + 1) * HALF)

        def blk(j):
            return slice(j * P, (j + 1) * P)

        def run(eng, program):
            program(None, None, 0, 1)
            program(None, 0, 1, 0)
            with eng.Fori(0, B - 3, 2) as i:
                program(i, i + 1, i + 2, 1)
                program(i + 1, i + 2, i + 3, 0)
            program(B - 2, B - 1, None, 1)
            program(B - 1, None, None, 0)

        block = ctx.enter_context(nc.Block())

        @block.sync
        def _(sp):
            def col(a):
                return a.rearrange("(p o) -> p o", o=1)

            def spread(a):
                return a.rearrange("(o b) -> o b", o=1).to_broadcast([P, B])

            def load_constants():
                sp.dma_start(w1[:, :, :], L1_W1.rearrange("(k p) a -> p k a", p=P)).then_inc(const_in, 16)
                sp.dma_start(b1_col[:, :], col(L1_b1)).then_inc(const_in, 16)
                sp.dma_start(v_col[:, :], col(L1_v)).then_inc(const_in, 16)
                for q, z in enumerate((condB_zX, condB_zY, condB_zR)):
                    sp.dma_start(raw3[:, q, :], spread(z)).then_inc(const_in, 16)
                sp.dma_start(tok_i[:, :], spread(itok_B_0_2)).then_inc(const_in, 16)

            def load_x(n, c):
                sl, r0, size = c % 2, c * 2 * P, 2 * P
                wait_past(sp, l0_done, NC * n + c - 1)

                def get(dst, lo, hi):
                    src = x[bass.ds(n, 1), lo:hi, :]
                    if hi - lo == size:
                        src = src.rearrange("b (j p) d -> p (b j) d", p=P)
                    else:
                        src = src.rearrange("b p d -> p (b d)")
                    sp.dma_start(dst, src).then_inc(x_loaded[sl], 16)

                get(xn[:, sl, :, 1:D + 1], r0, r0 + size)
                if c == 0:
                    get(xu[1:113, sl, 0, :], 0, 112)
                    get(xu[113:P, sl, 0, :], 112, P - 1)
                    get(xu[0:1, sl, 0, :], 1, 2)
                    get(xu[:, sl, 1, :], P - 1, 2 * P - 1)
                    get(xd[:, sl, :, :], r0 + 1, r0 + 1 + size)
                elif c == NC - 1:
                    get(xu[:, sl, :, :], r0 - 1, r0 - 1 + size)
                    get(xd[:, sl, 0, :], r0 + 1, r0 + 1 + P)
                    get(xd[0:112, sl, 1, :], r0 + P + 1, r0 + P + 113)
                    get(xd[112:P - 1, sl, 1, :], r0 + P + 113, S)
                    get(xd[P - 1:P, sl, 1, :], S - 2, S - 1)
                else:
                    get(xu[:, sl, :, :], r0 - 1, r0 - 1 + size)
                    get(xd[:, sl, :, :], r0 + 1, r0 + 1 + size)

            def token(tok, n, count):
                return sp.value_load(tok.rearrange("(o b) -> o b", o=1)[:, bass.ds(n, 1)],
                                     min_val=0, max_val=count - 1)

            def load_weights(n, q):
                subject = token(itok_B_0_7, n, NSUB)
                profile = token(itok_B_0_6, n, NPROF)
                wait_past(sp, wt_ps, 2 * n)
                wait_past(sp, bz_ps, n)
                sp.dma_start(wn[:, :, :], L2_w[bass.ds(subject, 1), :, :].rearrange(
                    "s (k p) h -> p (s k) h", p=P)).then_inc(wt_loaded, 16)
                sp.dma_start(wd[:, :, :], L3_dw[bass.ds(profile, 1), :, :].rearrange(
                    "s (k p) h -> p (s k) h", p=P)).then_inc(wt_loaded, 16)
                sp.dma_start(b_col[:, :], L2_b[bass.ds(subject, 1), :].rearrange(
                    "s (k p) -> p (s k)", p=P), allow_slow_non_contiguous=True).then_inc(wt_loaded, 16)
                wait_past(sp, bz_ready, n)
                sp.dma_start(bd_col[:, :], L3_db[bass.ds(profile, 1), :].rearrange("s p -> p s")
                             ).then_inc(wt_loaded, 16)
                wait_past(sp, bias_ready, n)
                sp.wait_ge(const_made, CONST_MADE)
                for i, (a, token_value) in enumerate(((L3_ub, profile), (L3_b, profile), (L2_b, subject))):
                    for p in (i, P // 2 + i):
                        sp.dma_start(rows[p:p + 1, :], a[bass.ds(token_value, 1), :]).then_inc(row_loaded, 16)
                wait_past(sp, wul_ready, n)
                sp.dma_start(wu[:, :], L3_uw[bass.ds(profile, 1), :, :].rearrange("s p h -> p (s h)")
                             ).then_inc(up_loaded, 16)
                wait_past(sp, y_free, NJ * (n - 1) + CREDIT)
                sp.dma_start(g_row[:, q, :], L3_g[bass.ds(profile, 1), :].to_broadcast([P, D])
                             ).then_inc(g_loaded, 16)

            def load(n, q):
                load_x(n, 0)
                load_x(n, 1)
                load_x(n, 2)
                load_x(n, 3)
                load_weights(n, q)

            load_constants()
            load(0, 0)
            with sp.Fori(1, B - 2, 2) as n:
                load(n, 1)
                load(n + 1, 0)
            load(B - 1, 1)

        @block.gpsimd
        def _(pool):
            own = [0]

            def link(ins):
                own[0] += 1
                ins.then_inc(pool_own, 1)
                pool.wait_ge(pool_own, own[0])

            def constants():
                link(pool.memset(ident[:, :], 0.0))
                pool.affine_select(out=ident[:, :], in_=ident[:, :], compare_op=ALU.not_equal, fill=1.0,
                                   base=0, pattern=[[-1, P]], channel_multiplier=1).then_inc(const_made, 1)
                link(pool.memset(masks[:, :, :], 0.0))
                for kind, (op, sign) in enumerate(((ALU.is_ge, 1), (ALU.is_ge, -1), (ALU.not_equal, 1))):
                    own_block = masks[:, kind, 0:P]
                    link(pool.affine_select(out=own_block, in_=own_block, compare_op=op, fill=BIG,
                                            base=0, pattern=[[-sign, P]], channel_multiplier=sign))
                for kind, (op, sign) in enumerate(((ALU.is_gt, 1), (ALU.is_gt, -1), (ALU.not_equal, 1))):
                    pairs = masks[:, kind, P:P + NB].rearrange("p (a b) -> p a b", b=NJ)
                    link(pool.affine_select(out=pairs, in_=pairs, compare_op=op, fill=BIG, base=0,
                                            pattern=[[sign, NJ], [-sign, NJ]], channel_multiplier=0))
                count = [masks[:, kind, P + NB:MASK] for kind in range(3)]
                link(pool.iota(iota_i[:, :], pattern=[[P, NJ]], base=1, channel_multiplier=1))
                link(pool.tensor_copy(count[0], iota_i[:, :]))
                link(pool.tensor_scalar(count[1], count[0], -1.0, float(S + 1), ALU.mult, ALU.add))
                pool.memset(count[2], float(S - 1)).then_inc(const_made, 1)
                link(pool.memset(ones[:, :], 1.0))
                link(pool.memset(minus_half[:, :], -0.5))
                link(pool.memset(rows[:, :], 0.0))
                link(pool.memset(rows_on_f[:, :, :], 0.0))
                for lo in (0, P // 2):
                    link(pool.memset(rows_on_f[lo:lo + 3, 0, :], 1.0))
                    link(pool.memset(rows_on_f[lo:lo + 1, 0, :], 0.0))
                    link(pool.memset(rows_on_f[lo:lo + 2, 1, :], -1.0))
                    link(pool.memset(rows_on_f[lo:lo + 1, 1, :], 1.0))
                pool.wait_ge(const_in, 16 * CONST_DMAS)
                pool.tensor_scalar(v_rep[:, :], ones[:, :], v_col[:, 0:1], 0.0, ALU.mult,
                                   ALU.add).then_inc(const_made, 2)

            def above_and_below(m, c):
                sl = c % 2
                pool.wait_ge(x_loaded[sl], x_count(m, c))
                pool.tensor_tensor(xu[:, sl, :, :], xu[:, sl, :, :], xd[:, sl, :, :],
                                   ALU.add).then_inc(pool_b, 1)

            def left_and_right(m, c):
                sl = c % 2
                pool.wait_ge(halo, NC * m + c + 1)
                pool.wait_ge(pool_b, NC * m + c + 1)
                pool.tensor_tensor(xd[:, sl, :, :], xn[:, sl, :, 0:D], xn[:, sl, :, 2:D + 2],
                                   ALU.add).then_inc(pool_a, 1)

            def bias_rest(n, q):
                pool.wait_ge(wul_ready, n + 1)
                pool.wait_ge(bias_h, n + 1)
                rest = bias[P // 2:P, q, :]
                pool.tensor_tensor(rest, rows[P // 2:P, :], rest.bitcast(F32),
                                   ALU.subtract).then_inc(bias_ready, 1)
                pool.wait_ge(bias_ready, n + 1)

            def root(b, t):
                r = t % OB
                pool.wait_ge(ve_ready, NJ * b + t + 1)
                pool.tensor_tensor(rstd[:, r:r + 1], ve[:, r:r + 1], minus_half[:, :],
                                   ALU.pow).then_inc(rstd_ready, 1)

            def finish(b, t):
                o = o_sb[:, t % OB, :]
                pool.wait_ge(scaled, NJ * b + t + 1)
                pool.wait_ge(x3_ready, NJ * b + t + 1)
                pool.tensor_tensor(o, o, x3[:, t % XB, :], ALU.add).then_inc(fin_done, 1)

            def rest_up(n, q):
                pool.wait_ge(wuh_ready, n + 1)
                pool.tensor_tensor(wul[:, q, :], wu[:, :], wuh[:, q, :].bitcast(F32),
                                   ALU.subtract).then_inc(wul_ready, 1)

            def rest_x2(n, q, k):
                pool.wait_ge(x2h_ready, KD * n + k + 1)
                pool.wait_ge(x2s, NG * (KD * n + k + 1))
                pool.tensor_tensor(x2l[q][:, k, :], x2f[:, k % 2, :], x2h[q][:, k, :].bitcast(F32),
                                   ALU.subtract).then_inc(x2l_ready, 1)

            def program(b, n, m, q):
                if m is not None:
                    above_and_below(m, 0)
                if b is not None:
                    root(b, 0)
                if m is not None:
                    left_and_right(m, 0)
                if b is not None:
                    root(b, 1)
                if m is not None:
                    above_and_below(m, 1)
                if n is not None:
                    rest_x2(n, q, 0)
                if b is not None:
                    finish(b, 0)
                    finish(b, 1)
                    root(b, 2)
                if m is not None:
                    left_and_right(m, 1)
                if b is not None:
                    root(b, 3)
                if n is not None:
                    rest_x2(n, q, 1)
                if b is not None:
                    finish(b, 2)
                if n is not None:
                    rest_x2(n, q, 2)
                if b is not None:
                    finish(b, 3)
                if n is not None:
                    rest_x2(n, q, 3)
                if b is not None:
                    root(b, 4)
                if m is not None:
                    above_and_below(m, 2)
                    left_and_right(m, 2)
                if b is not None:
                    finish(b, 4)
                if m is not None:
                    above_and_below(m, 3)
                    left_and_right(m, 3)
                if n is not None:
                    rest_up(n, q)
                    bias_rest(n, q)
                if b is not None:
                    root(b, 5)
                    finish(b, 5)
                    root(b, 6)
                    root(b, 7)
                    finish(b, 6)
                    finish(b, 7)

            constants()
            run(pool, program)

        @block.tensor
        def _(pe):
            mm = pe.matmul

            def split_product(dst, parts, first, last):
                for q, (lhs, rhs) in enumerate(parts):
                    ins = mm(dst, lhs, rhs, start=first and q == 0, stop=last and q == len(parts) - 1,
                             skip_group_check=True)
                return ins

            def transpose_x1(n, c):
                pe.wait_ge(l0_done, NC * n + c + 1)
                wait_past(pe, *((wtl_ready, 2 * n), (wtl_ready, 2 * n - 1), (x1t_ready, NC * n + 1),
                                (x1t_ready, NC * n + 2))[c])
                pair = (pair_a, pair_b)[c % 2]
                for k in range(KD):
                    for j in range(2):
                        ins = pe.transpose(pair[:, k * 2 * P + j * P:k * 2 * P + (j + 1) * P],
                                           x1[:, 2 * c + j, blk(k)], ident[:, :])
                ins.then_inc(xt_ps, 1)

            def score_hidden(n, q, h):
                pe.wait_ge(x1t_ready, NC * n + 2 * h + 2)
                if h == 0:
                    wait_past(pe, x2s, KD * NG * n)
                for k in range(KD):
                    ins = mm(hidden_ps[h], w1[:, k, :], x1t[q][:, k, half(h)],
                             start=k == 0, stop=k == KD - 1)
                ins.then_inc(h_ps, 1)

            def spread_scores(n, h):
                pe.wait_ge(th_ready, 2 * n + h + 1)
                mm(pair_b[:, half(h)], v_rep[:, :], th[:, half(h)], start=True, stop=True
                   ).then_inc(sc_ps, 1)

            def scores_by_row(n):
                pe.wait_ge(th_ready, 2 * n + 2)
                for j in range(NJ):
                    ins = mm(SN[:, j:j + 1], th[:, blk(j)], v_col[:, :], start=True, stop=True)
                ins.then_inc(sn_ps, 1)

            def down_through_w(n):
                pe.wait_ge(wn_ready, n + 1)
                pe.wait_ge(th_ready, 2 * n + 2)
                for hb in range(KD):
                    for ob in range(KD):
                        ins = mm(pair_a[:, blk(hb)], wn[:, ob, blk(hb)], wd[:, ob, :],
                                 start=ob == 0, stop=ob == KD - 1)
                ins.then_inc(v_ps, 1)
                for ob in range(KD):
                    ins = mm(BZ, wd[:, ob, :], b_col[:, ob:ob + 1], start=ob == 0, stop=ob == KD - 1)
                ins.then_inc(bz_ps, 1)

            def block_sums(n):
                pe.wait_ge(ex_ready, n + 1)
                mm(ZG, ones[:, :], E_ROW, start=True, stop=True).then_inc(g_ps, 1)

            def transpose_w(n, q):
                pe.wait_ge(*((x2s, KD * NG * (n + 1)), (zf_ready, 4 * n + 4))[q])
                pair = (pair_b, pair_a)[q]
                for hb in (2 * q, 2 * q + 1):
                    for ob in range(KD):
                        o = (hb % 2) * D + ob * P
                        ins = pe.transpose(pair[:, o:o + P], wn[:, ob, blk(hb)], ident[:, :])
                ins.then_inc(wt_ps, 1)

            def transpose_p(n):
                pe.wait_ge(pn_ready, n + 1)
                pe.wait_ge(vl_ready, n + 1)
                pe.wait_ge(bz_ready, n + 1)
                for j in range(NJ):
                    ins = pe.transpose(pair_a[:, blk(j)], pn[:, blk(j)], ident[:, :])
                ins.then_inc(pt_ps, 1)

            def transpose_alpha(n):
                pe.wait_ge(al_ready, n + 1)
                pe.wait_ge(sb_read, 2 * n + 2)
                for j in range(NJ):
                    ins = pe.transpose(pair_b[:, blk(j)], AL[:, j:j + 1].to_broadcast([P, P]), ident[:, :])
                ins.then_inc(al_ps, 1)

            def pool_blocks(n, k, groups):
                for g in groups:
                    j0, j1 = GROUPS[g]
                    last = [u for u in range(NG * k + g)
                            if GROUP_BANK[u // NG % 2][u % NG] == GROUP_BANK[k % 2][g]]
                    if last:
                        pe.wait_ge(x2s, KD * NG * n + last[-1] + 1)
                    else:
                        pe.wait_ge(*((pt_ready, n + 1) if k == 0 and g < 2 else (alb_ready, n + 1)))
                    for j in range(j0, j1):
                        o = (j - j0) * (P + 1)
                        ins = mm(front_ps[:, GROUP_BANK[k % 2][g], o:o + P + 1], x1[:, j, blk(k)],
                                 pt[:, j, :], start=True, stop=True)
                if g == NG - 1:
                    ins.then_inc(p_mm, 1)

            def adapter_down(n, q, h):
                if h == 0:
                    pe.wait_ge(x2s, KD * NG * n + 2 * NG + 2)
                    pe.wait_ge(vl_ready, n + 1)
                for k in range(KD):
                    if h == 0:
                        pe.wait_ge(x2l_ready, KD * n + k + 1)
                    ins = split_product(pair_a[:, half(h)], (
                        (vh[:, k, :], x2h[q][:, k, half(h)]), (vl[:, k, :], x2h[q][:, k, half(h)]),
                        (vh[:, k, :], x2l[q][:, k, half(h)])), k == 0, k == KD - 1)
                ins.then_inc(z_ps, 1)

            def linear(b, q, t):
                y = ys[t % YB]
                if t == 0:
                    pe.wait_ge(bias_ready, b + 1)
                pe.wait_ge(y_free, NJ * b + before(t, YB) + 1 + CREDIT)
                mm(y[:, :], rows_on[:, 0, :], bias[:, q, :], start=True, stop=False, skip_group_check=True)
                for k in range(KD):
                    if t == 0 and k % 2 == 0:
                        pe.wait_ge(wtl_ready, 2 * b + k // 2 + 1)
                    ins = split_product(y[:, :], (
                        (x2h[q][:, k, blk(t)], wth[:, k, :]), (x2h[q][:, k, blk(t)], wtl[:, k, :]),
                        (x2l[q][:, k, blk(t)], wth[:, k, :])), False, k == KD - 1)
                ins.then_inc(y_ps, 1)

            def adapter_up(b, q, t):
                y = ys[t % YB]
                pe.wait_ge(x3_ready, NJ * b + t + 1)
                if t == 0:
                    pe.wait_ge(wul_ready, b + 1)
                if t % (NJ // 2) == 0:
                    pe.wait_ge(zl_ready, 2 * b + t // (NJ // 2) + 1)
                mm(y[:, :], rows_on[:, 1, :], bias[:, q, :], start=False, stop=False, skip_group_check=True)
                ins = split_product(y[:, :], (
                    (zh[:, blk(t)], wuh[:, q, :]), (zh[:, blk(t)], wul[:, q, :]),
                    (zl[:, blk(t)], wuh[:, q, :])), False, True)
                ins.then_inc(u_ps, 1)

            def program(b, n, m, q):
                if n is not None:
                    spread_scores(n, 0)
                    spread_scores(n, 1)
                    scores_by_row(n)
                if b is not None:
                    linear(b, 1 - q, 0)
                    linear(b, 1 - q, 1)
                if n is not None:
                    block_sums(n)
                    down_through_w(n)
                    transpose_alpha(n)
                if b is not None:
                    adapter_up(b, 1 - q, 0)
                if n is not None:
                    transpose_p(n)
                if b is not None:
                    adapter_up(b, 1 - q, 1)
                if n is not None:
                    pool_blocks(n, 0, (0, 1))
                    pool_blocks(n, 0, (2,))
                    pool_blocks(n, 1, (0, 1))
                if b is not None:
                    linear(b, 1 - q, 2)
                if n is not None:
                    pool_blocks(n, 1, (2,))
                    pool_blocks(n, 2, (0, 1))
                if b is not None:
                    adapter_up(b, 1 - q, 2)
                    linear(b, 1 - q, 3)
                if n is not None:
                    pool_blocks(n, 2, (2,))
                    pool_blocks(n, 3, (0, 1))
                if b is not None:
                    adapter_up(b, 1 - q, 3)
                if n is not None:
                    pool_blocks(n, 3, (2,))
                if b is not None:
                    linear(b, 1 - q, 4)
                    linear(b, 1 - q, 5)
                    adapter_up(b, 1 - q, 4)
                    linear(b, 1 - q, 6)
                    adapter_up(b, 1 - q, 5)
                if n is not None:
                    adapter_down(n, q, 0)
                    adapter_down(n, q, 1)
                if b is not None:
                    linear(b, 1 - q, 7)
                    adapter_up(b, 1 - q, 6)
                    adapter_up(b, 1 - q, 7)
                if n is not None:
                    transpose_w(n, 0)
                    transpose_w(n, 1)
                if m is not None:
                    transpose_x1(m, 0)
                    transpose_x1(m, 1)
                    transpose_x1(m, 2)
                    transpose_x1(m, 3)
                    score_hidden(m, 1 - q, 0)
                    score_hidden(m, 1 - q, 1)

            pe.wait_ge(const_made, CONST_MADE)
            pe.wait_ge(table_made, 1)
            run(pe, program)

        @block.scalar
        def _(act):
            def copy(dst, src):
                return act.activation(dst, src, ACT.Identity)

            def reflect(m, c):
                sl = c % 2
                act.wait_ge(x_loaded[sl], x_count(m, c))
                copy(xn[:, sl, :, 0:D + 2:D + 1], xn[:, sl, :, 2:D:D - 3]).then_inc(halo, 1)

            def centre(m, c):
                act.wait_ge(x_loaded[c % 2], x_count(m, c))
                act.wait_ge(cur_ready, m + 1)
                wait_past(act, p_mm, KD * m)
                act.activation(x1[:, 2 * c:2 * c + 2, :], xn[:, c % 2, :, 1:D + 1], ACT.Identity,
                               bias=cur[:, CENTRE:CENTRE + 1], scale=cur[:, MINUS_R:MINUS_R + 1]
                               ).then_inc(c_done, 1)

            def keep_x1t(n, q, c):
                act.wait_ge(xt_ps, NC * n + c + 1)
                wait_past(act, y_ps, NJ * (n - 1))
                pair = (pair_a, pair_b)[c % 2]
                copy(x1t[q][:, :, c * 2 * P:(c + 1) * 2 * P],
                     pair[:, :].rearrange("p (k q) -> p k q", k=KD)).then_inc(x1t_ready, 1)

            def hidden(n, h):
                wait_past(act, p_mm, KD * n)
                act.wait_ge(h_ps, 2 * n + h + 1)
                act.activation(th[:, half(h)], hidden_ps[h], ACT.Tanh,
                               bias=b1_col[:, 0:1]).then_inc(th_ready, 1)

            def small_exps(n):
                act.wait_ge(arg_ready, n + 1)
                wait_past(act, g_ps, n)
                act.activation(EX, ARG, ACT.Exp).then_inc(ex_ready, 1)

            def row_exps(n):
                act.wait_ge(negm_ready, n + 1)
                for j in range(NJ):
                    ins = act.activation(pn[:, blk(j)], pn[:, blk(j)], ACT.Exp, bias=NEGM[:, j:j + 1],
                                         accum_out=ZD[:, j:j + 1])
                ins.then_inc(p_exp, 1)

            def round_v(n):
                act.wait_ge(v_ps, n + 1)
                wait_past(act, z_ps, 2 * n)
                copy(vh[:, :, :], pair_a[:, 0:KD * P].rearrange("p (k q) -> p k q", k=KD)
                     ).then_inc(vh_ready, 1)

            def round_w(n, q):
                act.wait_ge(wt_ps, 2 * n + q + 1)
                wait_past(act, y_ps, NJ * n)
                copy(wth[:, 2 * q:2 * q + 2, :], (pair_b, pair_a)[q].rearrange(
                    "p (k q) -> p k q", k=2)).then_inc(wth_ready, 1)

            def round_up(n, q):
                act.wait_ge(up_loaded, 16 * n + 16)
                wait_past(act, y_free, NJ * (n - 1) + CREDIT)
                copy(wuh[:, q, :], wu[:, :]).then_inc(wuh_ready, 1)

            def round_bias(n, q):
                act.wait_ge(row_loaded, 96 * n + 96)
                wait_past(act, y_free, NJ * (n - 1) + CREDIT)
                copy(bias[:, q, :], rows[:, :]).then_inc(bias_h, 1)

            def keep_p(n):
                act.wait_ge(pt_ps, n + 1)
                copy(pt[:, :, P], E_ROW)
                copy(pt[:, :, 0:P], pair_a.rearrange("p (j l) -> p j l", l=P)).then_inc(pt_ready, 1)

            def keep_alpha(n):
                act.wait_ge(al_ps, n + 1)
                wait_past(act, x2s, KD * NG * n)
                copy(alb[:, :], pair_b[:, :]).then_inc(alb_ready, 1)

            def round_x2(n, q, k):
                act.wait_ge(x2s, NG * (KD * n + k + 1))
                copy(x2h[q][:, k, :], x2f[:, k % 2, :]).then_inc(x2h_ready, 1)

            def adapter_relu(n, h):
                act.wait_ge(bz_ready, n + 1)
                act.wait_ge(z_ps, 2 * n + h + 1)
                wait_past(act, u_ps, NJ * n - NJ // 2 + h * (NJ // 2))
                act.activation(zf[:, half(h)], pair_a[:, half(h)], ACT.Relu,
                               bias=bz[:, 0:1]).then_inc(zf_ready, 1)
                act.activation(zh[:, half(h)], pair_a[:, half(h)], ACT.Relu,
                               bias=bz[:, 0:1]).then_inc(zf_ready, 1)

            def keep_x3(b, t):
                act.wait_ge(y_ps, NJ * b + t + 1)
                act.wait_ge(fin_done, NJ * b + before(t, XB) + 1 + CREDIT)
                copy(x3[:, t % XB, :], ys[t % YB][:, :]).then_inc(x3_ready, 1)

            def scale(b, t):
                o = o_sb[:, t % OB, :]
                act.wait_ge(rstd_ready, NJ * b + t + 1)
                act.wait_ge(y_free, NJ * b + t + 1 + CREDIT)
                act.activation(o, o, ACT.Identity, scale=rstd[:, t % OB:t % OB + 1]).then_inc(scaled, 1)

            def store(b, t):
                act.wait_ge(fin_done, NJ * b + t + 1 + CREDIT)
                act.dma_start(out[bass.ds(b, 1), blk(t), :].rearrange("b p d -> p (b d)"),
                              o_sb[:, t % OB, :]).then_inc(stored[t % OB], 16)

            def program(b, n, m, q):
                if n is not None:
                    small_exps(n)
                    row_exps(n)
                if b is not None:
                    keep_x3(b, 0)
                if n is not None:
                    round_v(n)
                if b is not None:
                    keep_x3(b, 1)
                if m is not None:
                    reflect(m, 0)
                if n is not None:
                    keep_alpha(n)
                    keep_p(n)
                if b is not None:
                    keep_x3(b, 2)
                    scale(b, 0)
                if n is not None:
                    round_x2(n, q, 0)
                if b is not None:
                    scale(b, 1)
                if m is not None:
                    reflect(m, 1)
                if b is not None:
                    keep_x3(b, 3)
                    scale(b, 2)
                if n is not None:
                    round_x2(n, q, 1)
                if b is not None:
                    store(b, 0)
                if m is not None:
                    centre(m, 0)
                if n is not None:
                    round_x2(n, q, 2)
                    round_bias(n, q)
                if m is not None:
                    centre(m, 1)
                if b is not None:
                    scale(b, 3)
                    keep_x3(b, 4)
                    store(b, 1)
                    store(b, 2)
                    keep_x3(b, 5)
                if n is not None:
                    round_x2(n, q, 3)
                if m is not None:
                    reflect(m, 2)
                if n is not None:
                    adapter_relu(n, 0)
                if b is not None:
                    keep_x3(b, 6)
                    scale(b, 4)
                if n is not None:
                    round_up(n, q)
                if m is not None:
                    centre(m, 2)
                if b is not None:
                    store(b, 3)
                    keep_x3(b, 7)
                    store(b, 4)
                if n is not None:
                    adapter_relu(n, 1)
                if m is not None:
                    reflect(m, 3)
                if n is not None:
                    round_w(n, 0)
                    round_w(n, 1)
                if m is not None:
                    centre(m, 3)
                    keep_x1t(m, 1 - q, 0)
                    keep_x1t(m, 1 - q, 1)
                if b is not None:
                    scale(b, 5)
                if m is not None:
                    keep_x1t(m, 1 - q, 2)
                    keep_x1t(m, 1 - q, 3)
                if b is not None:
                    scale(b, 6)
                if m is not None:
                    hidden(m, 0)
                if b is not None:
                    scale(b, 7)
                    store(b, 5)
                if m is not None:
                    hidden(m, 1)
                if b is not None:
                    store(b, 6)
                    store(b, 7)

            act.wait_ge(const_in, 16 * CONST_DMAS)
            run(act, program)
            for q in range(OB):
                act.wait_ge(stored[q], 16 * (B * NJ // OB) + 16)

        @block.vector
        def _(dve):
            opening = Chain(dve_opening, 3 + NC * 2)
            front = Chain(dve_front, 21)
            back = Chain(dve_back, NJ)

            def by_j(a):
                return a.rearrange("p (a b) -> p a b", b=NJ)

            def make_table():
                made = [0]

                def link(ins):
                    made[0] += 1
                    ins.then_inc(dve_setup, 1)
                    dve.wait_ge(dve_setup, made[0])

                dve.wait_ge(const_in, 16 * CONST_DMAS)
                zx, zy, zr = (raw3[:, q, :] for q in range(3))
                link(dve.tensor_copy(tok_f[:, :], tok_i[:, :]))
                link(dve.tensor_copy(table[:, Z_X:Z_Y + 1, :], raw3[:, 0:2, :]))
                link(dve.tensor_scalar(table[:, MINUS_R, :], zr, -1.0, None, ALU.mult))
                link(dve.tensor_scalar(table[:, IS_PREFIX, :], tok_f[:, :], 0.0, None, ALU.is_equal))
                link(dve.tensor_scalar(table[:, IS_POSTFIX, :], tok_f[:, :], 1.0, None, ALU.is_equal))
                centre, cloze = table[:, CENTRE, :], table[:, IS_CLOZE, :]
                link(dve.tensor_scalar(centre, zx, -2.0, 1.0, ALU.mult, ALU.add))
                link(dve.scalar_tensor_tensor(out=centre, in0=zy, scalar=-2.0, in1=centre,
                                              op0=ALU.mult, op1=ALU.add))
                link(dve.tensor_tensor(centre, centre, zr, ALU.add))
                link(dve.tensor_scalar(cloze, table[:, IS_PREFIX, :], -1.0, 1.0, ALU.mult, ALU.add))
                link(dve.tensor_tensor(cloze, cloze, table[:, IS_POSTFIX, :], ALU.subtract))
                dve.wait_ge(const_made, CONST_MADE)
                dve.tensor_copy(rows_on[:, :, :], rows_on_f[:, :, :]).then_inc(table_made, 1)

            def take_scalars(n):
                opening.start(n)
                wait_past(dve, c_done, NC * n)
                dve.tensor_copy(cur[:, :], table[:, :, bass.ds(n, 1)].rearrange("p a b -> p (a b)")
                                ).then_inc(cur_ready, 1)
                dve.wait_ge(cur_ready, n + 1)
                opening.mark(dve.tensor_scalar(mask[:, :], masks[:, 2, :], cur[:, IS_CLOZE:IS_CLOZE + 1],
                                             None, ALU.mult))
                for kind, col in ((1, IS_POSTFIX), (0, IS_PREFIX)):
                    opening.wait(dve)
                    opening.mark(dve.scalar_tensor_tensor(
                        out=mask[:, :], in0=masks[:, kind, :], scalar=cur[:, col:col + 1],
                        in1=mask[:, :], op0=ALU.mult, op1=ALU.add))

            def diffuse(n, c):
                sl = c % 2
                o = x1[:, 2 * c:2 * c + 2, :]
                dve.wait_ge(c_done, NC * n + c + 1)
                opening.mark(dve.tensor_tensor(o, o, xn[:, sl, :, 1:D + 1], ALU.mult))
                dve.wait_ge(pool_a, NC * n + c + 1)
                dve.wait_ge(pool_b, NC * n + c + 1)
                opening.wait(dve)
                opening.mark(dve.scalar_tensor_tensor(out=o, in0=xd[:, sl, :, :], scalar=cur[:, Z_X:Z_X + 1],
                                                    in1=o, op0=ALU.mult, op1=ALU.add))
                opening.wait(dve)
                dve.scalar_tensor_tensor(out=o, in0=xu[:, sl, :, :], scalar=cur[:, Z_Y:Z_Y + 1],
                                         in1=o, op0=ALU.mult, op1=ALU.add).then_inc(l0_done, 1)

            def add_identity(n):
                dve.wait_ge(wt_loaded, 64 * n + 64)
                diagonal = wn[:, :, :].rearrange("p k h -> p (k h)")
                for k in range(KD):
                    d = diagonal[:, k * (D + P):k * (D + P) + P]
                    ins = dve.tensor_tensor(d, d, ident[:, :], ALU.add)
                ins.then_inc(wn_ready, 1)

            def mask_scores(n, h):
                wait_past(dve, pt_ps, n)
                spread = pair_b[:, half(h)].rearrange("p (j l) -> p j l", l=P)
                own_mask = mask[:, 0:P].rearrange("p (o l) -> p o l", o=1).to_broadcast([P, NJ // 2, P])
                dve.wait_ge(sc_ps, 2 * n + h + 1)
                if h == 0:
                    front.start(n)
                front.mark(dve.tensor_tensor(pn[:, half(h)].rearrange("p (j l) -> p j l", l=P),
                                             spread, own_mask, ALU.add))
                dve.tensor_reduce(MI[:, 4 * h:4 * h + 4], spread, AX.X, ALU.max).then_inc(sb_read, 1)

            def maxima(n):
                front.wait(dve)
                front.mark(dve.tensor_reduce(MDIAG, pn[:, :].rearrange("p (j l) -> p j l", l=P),
                                             AX.X, ALU.max))
                dve.wait_ge(sb_read, 2 * n + 2)
                mi_all = MI.rearrange("p (o i) -> p o i", o=1).to_broadcast([P, NJ, NJ])
                front.mark(dve.tensor_tensor(by_j(KM), by_j(mask[:, P:P + NB]), mi_all, ALU.add))
                front.wait(dve)
                front.mark(dve.tensor_reduce(MCAR, by_j(KM), AX.X, ALU.max))
                dve.wait_ge(sn_ps, n + 1)
                front.mark(dve.tensor_tensor(ARG[:, 0:NJ], SN, MI, ALU.subtract))
                front.wait(dve)
                front.mark(dve.tensor_tensor(M, MDIAG, MCAR, ALU.max))
                mcar_all = MCAR.rearrange("p (j o) -> p j o", o=1).to_broadcast([P, NJ, NJ])
                front.mark(dve.tensor_tensor(by_j(ARG[:, NJ:NJ + NB]), by_j(KM), mcar_all, ALU.subtract))
                front.wait(dve)
                wait_past(dve, p_exp, n)
                dve.tensor_scalar(NEGM, M, -1.0, None, ALU.mult).then_inc(negm_ready, 1)
                dve.tensor_tensor(ARG[:, NJ + NB:], MCAR, M, ALU.subtract).then_inc(arg_ready, 1)

            def rest_v(n):
                dve.wait_ge(vh_ready, n + 1)
                dve.tensor_tensor(vl[:, :, :], pair_a[:, 0:KD * P].rearrange("p (k q) -> p k q", k=KD),
                                  vh[:, :, :].bitcast(F32), ALU.subtract).then_inc(vl_ready, 1)

            def block_weights(n):
                dve.wait_ge(g_ps, n + 1)
                dve.wait_ge(ex_ready, n + 1)
                front.mark(dve.tensor_tensor(prod[:, 0, :, :], ZG.rearrange("p (o i) -> p o i", o=1
                                             ).to_broadcast([P, NJ, NJ]), by_j(KAP), ALU.mult))
                front.wait(dve)
                dve.tensor_reduce(CC[:, 0:NJ], prod[:, 0, :, :], AX.X, ALU.add).then_inc(cc_ready, 1)

            def row_weights(n):
                dve.wait_ge(cc_ready, n + 1)
                front.mark(dve.tensor_tensor(ZT, ALH, CC[:, 0:NJ], ALU.mult))
                dve.wait_ge(p_exp, n + 1)
                front.wait(dve)
                front.mark(dve.tensor_tensor(ZT2, ZT, ZD, ALU.add))
                front.wait(dve)
                front.mark(dve.tensor_tensor(ZT, ZT2, mask[:, P + NB:MASK], ALU.mult))
                front.wait(dve)
                front.mark(dve.reciprocal(RZ, ZT))
                front.wait(dve)
                wait_past(dve, al_ps, n)
                dve.tensor_tensor(AL, ALH, RZ, ALU.mult).then_inc(al_ready, 1)

            def probabilities(n):
                for j in range(NJ):
                    ins = dve.scalar_tensor_tensor(out=pn[:, blk(j)], in0=pn[:, blk(j)],
                                                   scalar=RZ[:, j:j + 1], in1=ident[:, :],
                                                   op0=ALU.mult, op1=ALU.add)
                ins.then_inc(pn_ready, 1)

            def adapter_bias(n):
                dve.wait_ge(bz_ps, n + 1)
                wait_past(dve, zf_ready, 4 * n)
                dve.tensor_tensor(bz[:, :], BZ, bd_col[:, :], ALU.add).then_inc(bz_ready, 1)

            def rest_w(n, q):
                dve.wait_ge(wth_ready, 2 * n + q + 1)
                dve.tensor_tensor(wtl[:, 2 * q:2 * q + 2, :], (pair_b, pair_a)[q].rearrange(
                    "p (k q) -> p k q", k=2), wth[:, 2 * q:2 * q + 2, :].bitcast(F32),
                    ALU.subtract).then_inc(wtl_ready, 1)

            def carry_terms(n, k):
                dve.wait_ge(p_mm, KD * n + k + 1)
                for g, (j0, j1) in enumerate(GROUPS):
                    sums = front_ps[:, GROUP_BANK[k % 2][g], 0:(j1 - j0) * (P + 1)].rearrange(
                        "p (o i c) -> p o i c", o=1, c=P + 1)[:, :, :, P]
                    ins = dve.tensor_tensor(prod[:, k % 2, :, j0:j1], sums.to_broadcast([P, NJ, j1 - j0]),
                                            by_j(KAP)[:, :, j0:j1], ALU.mult)
                front.mark(ins)

            def add_carry(n, k):
                front.wait(dve)
                carry = CC[:, (k + 1) * NJ:(k + 2) * NJ]
                front.mark(dve.tensor_reduce(carry, prod[:, k % 2, :, :], AX.X, ALU.add))
                wait_past(dve, x2h_ready, KD * n + k - 1)
                wait_past(dve, x2l_ready, KD * n + k - 1)
                if k == 0:
                    dve.wait_ge(alb_ready, n + 1)
                    wait_past(dve, zl_ready, 2 * n)
                front.wait(dve)
                for g, (j0, j1) in enumerate(GROUPS):
                    for j in range(j0, j1):
                        o = (j - j0) * (P + 1)
                        ins = dve.scalar_tensor_tensor(
                            out=x2f[:, k % 2, blk(j)], in0=alb[:, blk(j)], scalar=carry[:, j:j + 1],
                            in1=front_ps[:, GROUP_BANK[k % 2][g], o:o + P], op0=ALU.mult, op1=ALU.add)
                    ins.then_inc(x2s, 1)

            def rest_z(n, h):
                dve.wait_ge(zf_ready, 4 * n + 2 * h + 2)
                dve.tensor_tensor(zl[:, half(h)], zf[:, half(h)], zh[:, half(h)].bitcast(F32),
                                  ALU.subtract).then_inc(zl_ready, 1)

            def moments(b, t):
                r = t % OB
                if t == 0:
                    back.start(b)
                dve.wait_ge(u_ps, NJ * b + t + 1)
                back.mark(dve.bn_stats(stats[:, r, :], ys[t % YB][:, :]))
                back.wait(dve)
                dve.memset(carrier[:, :], 0.0)
                dve.bn_aggr(mv[:, r, :], stats[:, r, :]).then_inc(mv_ready, 1)
                dve.wait_ge(mv_ready, NJ * b + t + 1)
                dve.wait_ge(stored[t % OB], 16 * (NJ // OB * b + t // OB) + 16)
                dve.tensor_scalar(ve[:, r:r + 1], mv[:, r, 1:2], EPS, None, ALU.add).then_inc(ve_ready, 1)

            def subtract_mean(b, q, t):
                dve.wait_ge(g_loaded, 16 * b + 16)
                dve.scalar_tensor_tensor(out=o_sb[:, t % OB, :], in0=ys[t % YB][:, :],
                                         scalar=mv[:, t % OB, 0:1], in1=g_row[:, q, :],
                                         op0=ALU.subtract, op1=ALU.mult).then_inc(y_free, 1)

            def program(b, n, m, q):
                if n is not None:
                    mask_scores(n, 0)
                    mask_scores(n, 1)
                    maxima(n)
                    add_identity(n)
                    block_weights(n)
                    row_weights(n)
                    probabilities(n)
                    rest_v(n)
                    adapter_bias(n)
                if b is not None:
                    moments(b, 0)
                if m is not None:
                    take_scalars(m)
                if b is not None:
                    moments(b, 1)
                    subtract_mean(b, 1 - q, 0)
                if n is not None:
                    carry_terms(n, 0)
                    add_carry(n, 0)
                if b is not None:
                    subtract_mean(b, 1 - q, 1)
                if n is not None:
                    carry_terms(n, 1)
                    add_carry(n, 1)
                if b is not None:
                    moments(b, 2)
                    subtract_mean(b, 1 - q, 2)
                if n is not None:
                    carry_terms(n, 2)
                    add_carry(n, 2)
                if b is not None:
                    moments(b, 3)
                if n is not None:
                    carry_terms(n, 3)
                if b is not None:
                    subtract_mean(b, 1 - q, 3)
                if m is not None:
                    diffuse(m, 0)
                if n is not None:
                    add_carry(n, 3)
                if b is not None:
                    moments(b, 4)
                if m is not None:
                    diffuse(m, 1)
                if b is not None:
                    subtract_mean(b, 1 - q, 4)
                    moments(b, 5)
                if m is not None:
                    diffuse(m, 2)
                if n is not None:
                    rest_z(n, 0)
                if b is not None:
                    subtract_mean(b, 1 - q, 5)
                if n is not None:
                    rest_w(n, 0)
                    rest_w(n, 1)
                if m is not None:
                    diffuse(m, 3)
                if b is not None:
                    moments(b, 6)
                    subtract_mean(b, 1 - q, 6)
                    moments(b, 7)
                    subtract_mean(b, 1 - q, 7)
                if n is not None:
                    rest_z(n, 1)
                if n is not None:
                    front.end()
                if m is not None:
                    opening.end()

            dve.sem_inc(y_free, CREDIT)
            dve.sem_inc(fin_done, CREDIT)
            for slot in range(OB):
                dve.sem_inc(stored[slot], 16)
            make_table()
            run(dve, program)


_INS = ["x", "condB_zX", "condB_zY", "condB_zR", "itok_B_0_2", "itok_B_0_7", "itok_B_0_6",
        "L1_cond_W1", "L1_cond_b1", "L1_cond_v", "L2_cond_weight", "L2_cond_bias", "L3_cond_down_w",
        "L3_cond_down_b", "L3_cond_up_w", "L3_cond_up_b", "L3_cond_ln_g", "L3_cond_ln_b"]


def kernel(**inputs):
    import concourse.bacc as bacc
    from concourse.bass_utils import run_bass_kernel_spmd

    nc = bacc.Bacc("TRN2", target_bir_lowering=False, num_devices=1)
    arrays, args = {}, []
    for name in _INS:
        a = np.ascontiguousarray(inputs[name])
        arrays[f"in_{name}"] = a
        args.append(nc.dram_tensor(f"in_{name}", a.shape, mybir.dt.from_np(a.dtype),
                                   kind="ExternalInput").ap())
    out = nc.dram_tensor("out_0", inputs["x"].shape, F32, kind="ExternalOutput").ap()
    build(nc, *args, out)
    return run_bass_kernel_spmd(nc, [arrays], core_ids=[0]).results[0]["out_0"]
```

```python
from contextlib import ExitStack

import numpy as np
import concourse.bass as bass
from concourse import mybir

F32 = mybir.dt.float32
F32R = mybir.dt.float32r
I32 = mybir.dt.int32
ALU = mybir.AluOpType
ACT = mybir.ActivationFunctionType
AX = mybir.AxisListType

P = 128
BIG = -1.0e30
EPS = 1e-5
TABLE = 7
Z_X, Z_Y, CENTRE, MINUS_R, IS_PREFIX, IS_POSTFIX, IS_CLOZE = range(7)


def wait_past(eng, sem, count):
    if isinstance(count, int) and count <= 0:
        return
    eng.wait_ge(sem, count)


class Chain:

    def __init__(self, sem, per_batch):
        self.sem, self.per_batch, self.n = sem, per_batch, 0

    def start(self):
        assert self.n in (0, self.per_batch)
        self.n = 0

    def mark(self, ins):
        ins.then_inc(self.sem, 1)
        self.n += 1

    def wait(self, eng, batch):
        eng.wait_ge(self.sem, batch * self.per_batch + self.n)


def build(nc, x, condB_zX, condB_zY, condB_zR, itok_B_0_2, itok_B_0_7, itok_B_0_6,
          L1_W1, L1_b1, L1_v, L2_w, L2_b, L3_dw, L3_db, L3_uw, L3_ub, L3_g, L3_b, out):
    B, S, D = x.shape
    A = L1_W1.shape[1]
    NJ = S // P
    KD = D // P
    NC = NJ // 2
    NSUB, NPROF = L2_w.shape[0], L3_dw.shape[0]
    assert A == P and NJ == 8 and KD == 4
    HALF = S // 2
    NB = NJ * NJ
    MASK = P + NB + NJ
    YB, XB, OB = 3, 3, 4

    with ExitStack() as ctx:
        def sb(name, shape, dt=F32):
            return ctx.enter_context(nc.sbuf_tensor(name, shape, dt))

        def ps(name, cols):
            return ctx.enter_context(nc.psum_tensor(name, [P, cols], F32))

        def sem(name):
            return ctx.enter_context(nc.semaphore(name))

        ident = sb("ident", [P, P])
        masks = sb("masks", [P, 3, MASK])
        rows_on = sb("rows_on", [P, 2, P], F32R)
        ones = sb("ones", [P, P])
        v_rep = sb("v_rep", [P, P])
        v_col = sb("v_col", [P, 1])
        b1_col = sb("b1_col", [P, 1])
        w1 = sb("w1", [P, KD, A])
        raw3 = sb("raw3", [P, 3, B])
        iota_i = sb("iota_i", [P, NJ], I32)
        tok_i = sb("tok_i", [P, B], I32)
        tok_f = sb("tok_f", [P, B])
        table = sb("table", [P, TABLE, B])
        xn = sb("xn", [P, 2, 2, D + 2])
        xu = sb("xu", [P, 2, 2, D])
        xd = sb("xd", [P, 2, 2, D])
        x1 = sb("x1", [P, NJ, D])
        cur = sb("cur", [P, TABLE])
        mask = sb("mask", [P, MASK])
        pn = sb("pn", [P, S])
        th_pt = sb("th_pt", [P, NJ, P + 1])
        th, pt = th_pt[:, :, :].rearrange("p j l -> p (j l)")[:, 0:S], th_pt
        alb = sb("alb", [P, S])
        rows_on_f = pn[:, 0:2 * P].rearrange("p (i m) -> p i m", i=2)
        small = sb("small", [P, 3 * P])
        prod = sb("prod", [P, 2, NJ, NJ])
        x2f = sb("x2f", [P, 2, S])
        x1t, x2h, x2l = [], [], []
        for q in range(2):
            with nc.sbuf_tensor(f"x1t{q}", [P, KD, S], F32) as a:
                x1t.append(a)
            x2l.append(sb(f"x2l{q}", [P, KD, S], F32R))
            x2h.append(sb(f"x2h{q}", [P, KD, S], F32R))
        wn = sb("wn", [P, KD, D])
        wth = sb("wth", [P, KD, D], F32R)
        wtl = sb("wtl", [P, KD, D], F32R)
        wd = sb("wd", [P, KD, P])
        vh = sb("vh", [P, KD, P], F32R)
        vl = sb("vl", [P, KD, P], F32R)
        wu = sb("wu", [P, D])
        wuh = sb("wuh", [P, 2, D], F32R)
        wul = sb("wul", [P, 2, D], F32R)
        b_col = sb("b_col", [P, KD])
        bd_col = sb("bd_col", [P, 1])
        bz = sb("bz", [P, 1])
        rows = sb("rows", [P, D])
        bias = sb("bias", [P, 2, D], F32R)
        g_row = sb("g_row", [P, 2, D])
        zf = x2f[:, 0, :]
        zh = sb("zh", [P, S], F32R)
        zl = sb("zl", [P, S], F32R)
        x3 = sb("x3", [P, XB, D])
        o_sb = sb("o_sb", [P, OB, D])
        stats = sb("stats", [P, OB, 6])
        mv = sb("mv", [P, OB, 2])
        ve = sb("ve", [P, OB])
        minus_half = sb("minus_half", [P, 1])
        rstd = sb("rstd", [P, OB])
        carrier = sb("carrier", [P, 1])

        ys = [ps(f"y{i}", D) for i in range(YB)]
        NF = 5
        front_ps = ctx.enter_context(nc.psum_tensor("front_ps", [P, NF, 512], F32))
        pair_a = front_ps[:, 0:2, :].rearrange("p b n -> p (b n)")
        pair_b = front_ps[:, 2:4, :].rearrange("p b n -> p (b n)")
        cbank = front_ps[:, 4, :]
        hidden_ps = (cbank, pair_a[:, 0:512])
        SN, ZG = cbank[:, 0:NJ], cbank[:, NJ:2 * NJ]
        BZ = pair_a[:, 512:513]
        GROUPS = ((0, 3), (3, 6), (6, 8))
        GROUP_BANK = ((0, 1, 2), (3, 4, 2))
        GROUP_ORDER = (2, 0, 1)
        NG = len(GROUPS)

        off = [0]

        def cols(n):
            off[0] += n
            return small[:, off[0] - n:off[0]]

        MI = cols(NJ)
        MDIAG, MCAR, M, NEGM = cols(NJ), cols(NJ), cols(NJ), cols(NJ)
        KM = cols(NB)
        ARG = cols(2 * NJ + NB)
        EX = cols(2 * NJ + NB)
        E_ROW, KAP, ALH = EX[:, 0:NJ], EX[:, NJ:NJ + NB], EX[:, NJ + NB:]
        ZD, CC, ZT, RZ, AL = cols(NJ), cols((KD + 1) * NJ), cols(NJ), cols(NJ), cols(NJ)
        ZT2 = cols(NJ)

        const_in = sem("const_in")
        const_made = sem("const_made")
        table_made = sem("table_made")
        cur_ready = sem("cur_ready")
        wt_loaded = sem("wt_loaded")
        row_loaded = sem("row_loaded")
        up_loaded = sem("up_loaded")
        halo = sem("halo")
        c_done = sem("c_done")
        pool_a = sem("pool_a")
        pool_b = sem("pool_b")
        scaled_rows = sem("scaled_rows")
        around = sem("around")
        own_done = sem("own_done")
        l0_done = sem("l0_done")
        xt_ps = sem("xt_ps")
        x1t_ready = sem("x1t_ready")
        h_ps = sem("h_ps")
        th_ready = sem("th_ready")
        sc_ps = sem("sc_ps")
        sn_ps = sem("sn_ps")
        sb_read = sem("sb_read")
        arg_ready = sem("arg_ready")
        ex_ready = sem("ex_ready")
        negm_ready = sem("negm_ready")
        p_exp = sem("p_exp")
        g_ps = sem("g_ps")
        cc_ready = sem("cc_ready")
        al_ready = sem("al_ready")
        pn_ready = sem("pn_ready")
        al_ps = sem("al_ps")
        pt_ps = sem("pt_ps")
        alb_ready = sem("alb_ready")
        pt_ready = sem("pt_ready")
        p_mm = sem("p_mm")
        x2s = sem("x2s")
        x2h_ready = sem("x2h_ready")
        x2l_ready = sem("x2l_ready")
        wn_ready = sem("wn_ready")
        v_ps = sem("v_ps")
        vh_ready = sem("vh_ready")
        vl_ready = sem("vl_ready")
        bz_ps = sem("bz_ps")
        bz_ready = sem("bz_ready")
        wt_ps = sem("wt_ps")
        wth_ready = sem("wth_ready")
        wtl_ready = sem("wtl_ready")
        wuh_ready = sem("wuh_ready")
        wul_ready = sem("wul_ready")
        bias_h = sem("bias_h")
        bias_ready = sem("bias_ready")
        g_loaded = sem("g_loaded")
        z_ps = sem("z_ps")
        zf_ready = sem("zf_ready")
        zl_ready = sem("zl_ready")
        y_ps = sem("y_ps")
        x3_ready = sem("x3_ready")
        u_ps = sem("u_ps")
        y_free = sem("y_free")
        mv_ready = sem("mv_ready")
        ve_ready = sem("ve_ready")
        rstd_ready = sem("rstd_ready")
        scaled = sem("scaled")
        fin_done = sem("fin_done")
        dve_opening = sem("dve_opening")
        dve_front = sem("dve_front")
        dve_back = sem("dve_back")
        dve_setup = sem("dve_setup")
        pool_own = sem("pool_own")
        x_loaded = [sem("x_loaded0"), sem("x_loaded1")]
        stored = [sem(f"stored{i}") for i in range(OB)]

        CREDIT = NJ
        CONST_DMAS, CONST_MADE = 7, 4

        X_DMAS = [6] + [3] * (NC - 2) + [6]

        def x_count(n, c):
            return n * 16 * sum(X_DMAS[c % 2::2]) + 16 * sum(X_DMAS[c % 2:c + 1:2])

        def before(t, ring):
            return t - ring if t >= ring else max(u for u in range(NJ) if u % ring == t % ring) - NJ

        def half(h):
            return slice(h * HALF, (h + 1) * HALF)

        def blk(j):
            return slice(j * P, (j + 1) * P)

        def run(eng, program):
            program(None, None, 0, 1)
            program(None, 0, 1, 0)
            with eng.Fori(0, B - 3, 2) as i:
                program(i, i + 1, i + 2, 1)
                program(i + 1, i + 2, i + 3, 0)
            program(B - 2, B - 1, None, 1)
            program(B - 1, None, None, 0)

        block = ctx.enter_context(nc.Block())

        @block.sync
        def _(sp):
            def col(a):
                return a.rearrange("(p o) -> p o", o=1)

            def spread(a):
                return a.rearrange("(o b) -> o b", o=1).to_broadcast([P, B])

            def load_constants():
                sp.dma_start(w1[:, :, :], L1_W1.rearrange("(k p) a -> p k a", p=P)).then_inc(const_in, 16)
                sp.dma_start(b1_col[:, :], col(L1_b1)).then_inc(const_in, 16)
                sp.dma_start(v_col[:, :], col(L1_v)).then_inc(const_in, 16)
                for q, z in enumerate((condB_zX, condB_zY, condB_zR)):
                    sp.dma_start(raw3[:, q, :], spread(z)).then_inc(const_in, 16)
                sp.dma_start(tok_i[:, :], spread(itok_B_0_2)).then_inc(const_in, 16)

            def load_x(n, c):
                sl, r0, size = c % 2, c * 2 * P, 2 * P
                wait_past(sp, l0_done, NC * n + c - 1)

                def get(dst, lo, hi):
                    src = x[bass.ds(n, 1), lo:hi, :]
                    if hi - lo == size:
                        src = src.rearrange("b (j p) d -> p (b j) d", p=P)
                    else:
                        src = src.rearrange("b p d -> p (b d)")
                    sp.dma_start(dst, src).then_inc(x_loaded[sl], 16)

                get(xn[:, sl, :, 1:D + 1], r0, r0 + size)
                if c == 0:
                    get(xu[1:113, sl, 0, :], 0, 112)
                    get(xu[113:P, sl, 0, :], 112, P - 1)
                    get(xu[0:1, sl, 0, :], 1, 2)
                    get(xu[:, sl, 1, :], P - 1, 2 * P - 1)
                    get(xd[:, sl, :, :], r0 + 1, r0 + 1 + size)
                elif c == NC - 1:
                    get(xu[:, sl, :, :], r0 - 1, r0 - 1 + size)
                    get(xd[:, sl, 0, :], r0 + 1, r0 + 1 + P)
                    get(xd[0:112, sl, 1, :], r0 + P + 1, r0 + P + 113)
                    get(xd[112:P - 1, sl, 1, :], r0 + P + 113, S)
                    get(xd[P - 1:P, sl, 1, :], S - 2, S - 1)
                else:
                    get(xu[:, sl, :, :], r0 - 1, r0 - 1 + size)
                    get(xd[:, sl, :, :], r0 + 1, r0 + 1 + size)

            def token(tok, n, count):
                return sp.value_load(tok.rearrange("(o b) -> o b", o=1)[:, bass.ds(n, 1)],
                                     min_val=0, max_val=count - 1)

            def load_weights(n, q):
                subject = token(itok_B_0_7, n, NSUB)
                profile = token(itok_B_0_6, n, NPROF)
                wait_past(sp, wt_ps, 2 * n)
                wait_past(sp, bz_ps, n)
                sp.dma_start(wn[:, :, :], L2_w[bass.ds(subject, 1), :, :].rearrange(
                    "s (k p) h -> p (s k) h", p=P)).then_inc(wt_loaded, 16)
                sp.dma_start(wd[:, :, :], L3_dw[bass.ds(profile, 1), :, :].rearrange(
                    "s (k p) h -> p (s k) h", p=P)).then_inc(wt_loaded, 16)
                sp.dma_start(b_col[:, :], L2_b[bass.ds(subject, 1), :].rearrange(
                    "s (k p) -> p (s k)", p=P), allow_slow_non_contiguous=True).then_inc(wt_loaded, 16)
                wait_past(sp, bz_ready, n)
                sp.dma_start(bd_col[:, :], L3_db[bass.ds(profile, 1), :].rearrange("s p -> p s")
                             ).then_inc(wt_loaded, 16)
                wait_past(sp, bias_ready, n)
                sp.wait_ge(table_made, 1)
                for i, (a, token_value) in enumerate(((L3_ub, profile), (L3_b, profile), (L2_b, subject))):
                    for p in (i, P // 2 + i):
                        sp.dma_start(rows[p:p + 1, :], a[bass.ds(token_value, 1), :]).then_inc(row_loaded, 16)
                wait_past(sp, wul_ready, n)
                sp.dma_start(wu[:, :], L3_uw[bass.ds(profile, 1), :, :].rearrange("s p h -> p (s h)")
                             ).then_inc(up_loaded, 16)
                wait_past(sp, y_free, NJ * (n - 1) + CREDIT)
                sp.dma_start(g_row[:, q, :], L3_g[bass.ds(profile, 1), :].to_broadcast([P, D])
                             ).then_inc(g_loaded, 16)

            def load(n, q):
                load_x(n, 0)
                load_x(n, 1)
                load_x(n, 2)
                load_x(n, 3)
                load_weights(n, q)

            load_x(0, 0)
            load_constants()
            for c in range(1, NC):
                load_x(0, c)
            load_weights(0, 0)
            with sp.Fori(1, B - 2, 2) as n:
                load(n, 1)
                load(n + 1, 0)
            load(B - 1, 1)

        @block.gpsimd
        def _(pool):
            own = [0]

            def link(ins):
                own[0] += 1
                ins.then_inc(pool_own, 1)
                pool.wait_ge(pool_own, own[0])

            def constants():
                link(pool.memset(ident[:, :], 0.0))
                pool.affine_select(out=ident[:, :], in_=ident[:, :], compare_op=ALU.not_equal, fill=1.0,
                                   base=0, pattern=[[-1, P]], channel_multiplier=1).then_inc(const_made, 1)
                link(pool.memset(masks[:, :, :], 0.0))
                for kind, (op, sign) in enumerate(((ALU.is_ge, 1), (ALU.is_ge, -1), (ALU.not_equal, 1))):
                    own_block = masks[:, kind, 0:P]
                    link(pool.affine_select(out=own_block, in_=own_block, compare_op=op, fill=BIG,
                                            base=0, pattern=[[-sign, P]], channel_multiplier=sign))
                for kind, (op, sign) in enumerate(((ALU.is_gt, 1), (ALU.is_gt, -1), (ALU.not_equal, 1))):
                    pairs = masks[:, kind, P:P + NB].rearrange("p (a b) -> p a b", b=NJ)
                    link(pool.affine_select(out=pairs, in_=pairs, compare_op=op, fill=BIG, base=0,
                                            pattern=[[sign, NJ], [-sign, NJ]], channel_multiplier=0))
                count = [masks[:, kind, P + NB:MASK] for kind in range(3)]
                link(pool.iota(iota_i[:, :], pattern=[[P, NJ]], base=1, channel_multiplier=1))
                link(pool.tensor_copy(count[0], iota_i[:, :]))
                link(pool.tensor_scalar(count[1], count[0], -1.0, float(S + 1), ALU.mult, ALU.add))
                pool.memset(count[2], float(S - 1)).then_inc(const_made, 1)
                link(pool.memset(ones[:, :], 1.0))
                link(pool.memset(minus_half[:, :], -0.5))
                pool.wait_ge(const_in, 16 * CONST_DMAS)
                pool.tensor_scalar(v_rep[:, :], ones[:, :], v_col[:, 0:1], 0.0, ALU.mult,
                                   ALU.add).then_inc(const_made, 2)

            def above_and_below(m, c):
                sl = c % 2
                pool.wait_ge(x_loaded[sl], x_count(m, c))
                pool.tensor_tensor(xu[:, sl, :, :], xu[:, sl, :, :], xd[:, sl, :, :],
                                   ALU.add).then_inc(pool_b, 1)

            def left_and_right(m, c):
                sl = c % 2
                pool.wait_ge(halo, NC * m + c + 1)
                pool.wait_ge(pool_b, NC * m + c + 1)
                pool.tensor_tensor(xd[:, sl, :, :], xn[:, sl, :, 0:D], xn[:, sl, :, 2:D + 2],
                                   ALU.add).then_inc(pool_a, 1)

            def bias_rest(n, q):
                pool.wait_ge(wul_ready, n + 1)
                pool.wait_ge(bias_h, n + 1)
                rest = bias[P // 2:P, q, :]
                pool.tensor_tensor(rest, rows[P // 2:P, :], rest.bitcast(F32),
                                   ALU.subtract).then_inc(bias_ready, 1)
                pool.wait_ge(bias_ready, n + 1)

            def root(b, t):
                r = t % OB
                pool.wait_ge(ve_ready, NJ * b + t + 1)
                pool.tensor_tensor(rstd[:, r:r + 1], ve[:, r:r + 1], minus_half[:, :],
                                   ALU.pow).then_inc(rstd_ready, 1)

            def finish(b, t):
                o = o_sb[:, t % OB, :]
                pool.wait_ge(scaled, NJ * b + t + 1)
                pool.wait_ge(x3_ready, NJ * b + t + 1)
                pool.tensor_tensor(o, o, x3[:, t % XB, :], ALU.add).then_inc(fin_done, 1)

            def rest_up(n, q):
                pool.wait_ge(wuh_ready, n + 1)
                pool.tensor_tensor(wul[:, q, :], wu[:, :], wuh[:, q, :].bitcast(F32),
                                   ALU.subtract).then_inc(wul_ready, 1)

            def rest_x2(n, q, k):
                pool.wait_ge(x2h_ready, KD * n + k + 1)
                pool.wait_ge(x2s, NG * (KD * n + k + 1))
                pool.tensor_tensor(x2l[q][:, k, :], x2f[:, k % 2, :], x2h[q][:, k, :].bitcast(F32),
                                   ALU.subtract).then_inc(x2l_ready, 1)

            def program(b, n, m, q):
                if b is not None:
                    root(b, 0)
                    root(b, 1)
                    finish(b, 0)
                if n is not None:
                    rest_up(n, q)
                    bias_rest(n, q)
                if m is not None:
                    above_and_below(m, 0)
                    left_and_right(m, 0)
                if b is not None:
                    finish(b, 1)
                if m is not None:
                    above_and_below(m, 1)
                    left_and_right(m, 1)
                if b is not None:
                    root(b, 2)
                if n is not None:
                    rest_x2(n, q, 0)
                if b is not None:
                    finish(b, 2)
                    root(b, 3)
                    root(b, 4)
                if n is not None:
                    rest_x2(n, q, 1)
                if b is not None:
                    finish(b, 3)
                    finish(b, 4)
                if n is not None:
                    rest_x2(n, q, 2)
                    rest_x2(n, q, 3)
                if m is not None:
                    above_and_below(m, 2)
                    left_and_right(m, 2)
                if b is not None:
                    root(b, 5)
                    root(b, 6)
                if m is not None:
                    above_and_below(m, 3)
                    left_and_right(m, 3)
                if b is not None:
                    root(b, 7)
                    finish(b, 5)
                    finish(b, 6)
                    finish(b, 7)

            constants()
            run(pool, program)

        @block.tensor
        def _(pe):
            mm = pe.matmul

            def split_product(dst, parts, first, last):
                for q, (lhs, rhs) in enumerate(parts):
                    ins = mm(dst, lhs, rhs, start=first and q == 0, stop=last and q == len(parts) - 1,
                             skip_group_check=True)
                return ins

            def transpose_x1(n, c):
                pe.wait_ge(l0_done, NC * n + c + 1)
                wait_past(pe, *((wtl_ready, 2 * n - 1), (wtl_ready, 2 * n), (x1t_ready, NC * n + 1),
                                (x1t_ready, NC * n + 2))[c])
                pair = (pair_b, pair_a)[c % 2]
                for k in range(KD):
                    for j in range(2):
                        ins = pe.transpose(pair[:, k * 2 * P + j * P:k * 2 * P + (j + 1) * P],
                                           x1[:, 2 * c + j, blk(k)], ident[:, :])
                ins.then_inc(xt_ps, 1)

            def score_hidden(n, q, h):
                pe.wait_ge(x1t_ready, NC * n + 2 * h + 2)
                if h == 0:
                    wait_past(pe, x2s, KD * NG * n)
                for k in range(KD):
                    ins = mm(hidden_ps[h], w1[:, k, :], x1t[q][:, k, half(h)],
                             start=k == 0, stop=k == KD - 1)
                ins.then_inc(h_ps, 1)

            def spread_scores(n, h):
                pe.wait_ge(th_ready, 2 * n + h + 1)
                pe.wait_ge(x1t_ready, NC * n + 3)
                mm(pair_b[:, half(h)], v_rep[:, :], th[:, half(h)], start=True, stop=True
                   ).then_inc(sc_ps, 1)

            def scores_by_row(n):
                pe.wait_ge(th_ready, 2 * n + 2)
                for j in range(NJ):
                    ins = mm(SN[:, j:j + 1], th[:, blk(j)], v_col[:, :], start=True, stop=True)
                ins.then_inc(sn_ps, 1)

            def down_through_w(n):
                pe.wait_ge(wn_ready, n + 1)
                pe.wait_ge(th_ready, 2 * n + 2)
                for hb in range(KD):
                    for ob in range(KD):
                        ins = mm(pair_a[:, blk(hb)], wn[:, ob, blk(hb)], wd[:, ob, :],
                                 start=ob == 0, stop=ob == KD - 1)
                ins.then_inc(v_ps, 1)
                for ob in range(KD):
                    ins = mm(BZ, wd[:, ob, :], b_col[:, ob:ob + 1], start=ob == 0, stop=ob == KD - 1)
                ins.then_inc(bz_ps, 1)

            def block_sums(n):
                pe.wait_ge(ex_ready, n + 1)
                mm(ZG, ones[:, :], E_ROW, start=True, stop=True).then_inc(g_ps, 1)

            def transpose_w(n, q):
                pe.wait_ge(*((x2s, KD * NG * (n + 1)), (zf_ready, 4 * n + 4))[q])
                pair = (pair_b, pair_a)[q]
                for hb in (2 * q, 2 * q + 1):
                    for ob in range(KD):
                        o = (hb % 2) * D + ob * P
                        ins = pe.transpose(pair[:, o:o + P], wn[:, ob, blk(hb)], ident[:, :])
                ins.then_inc(wt_ps, 1)

            def transpose_p(n, h):
                pe.wait_ge(pn_ready, 2 * n + h + 1)
                pe.wait_ge(vl_ready, n + 1)
                pe.wait_ge(bz_ready, n + 1)
                for j in range(4 * h, 4 * h + 4):
                    ins = pe.transpose(pair_a[:, blk(j)], pn[:, blk(j)], ident[:, :])
                ins.then_inc(pt_ps, 1)

            def transpose_alpha(n):
                pe.wait_ge(al_ready, n + 1)
                pe.wait_ge(sb_read, 2 * n + 2)
                for j in range(NJ):
                    ins = pe.transpose(pair_b[:, blk(j)], AL[:, j:j + 1].to_broadcast([P, P]), ident[:, :])
                ins.then_inc(al_ps, 1)

            def pool_blocks(n, k, groups):
                for g in groups:
                    j0, j1 = GROUPS[g]
                    last = [NG * u + GROUP_ORDER.index(v) for u in range(k) for v in range(NG)
                            if GROUP_BANK[u % 2][v] == GROUP_BANK[k % 2][g]]
                    if last:
                        pe.wait_ge(x2s, KD * NG * n + max(last) + 1)
                    elif k == 0 and g < 2:
                        pe.wait_ge(pt_ready, 2 * n + g + 1)
                    else:
                        pe.wait_ge(alb_ready, n + 1)
                    for j in range(j0, j1):
                        o = (j - j0) * (P + 1)
                        ins = mm(front_ps[:, GROUP_BANK[k % 2][g], o:o + P + 1], x1[:, j, blk(k)],
                                 pt[:, j, :], start=True, stop=True)
                if g == NG - 1:
                    ins.then_inc(p_mm, 1)

            def adapter_down(n, q, h):
                if h == 0:
                    pe.wait_ge(x2s, KD * NG * n + 3 * NG)
                    pe.wait_ge(vl_ready, n + 1)
                for k in range(KD):
                    if h == 0:
                        pe.wait_ge(x2l_ready, KD * n + k + 1)
                    ins = split_product(pair_a[:, half(h)], (
                        (vh[:, k, :], x2h[q][:, k, half(h)]), (vl[:, k, :], x2h[q][:, k, half(h)]),
                        (vh[:, k, :], x2l[q][:, k, half(h)])), k == 0, k == KD - 1)
                ins.then_inc(z_ps, 1)

            def linear(b, q, t):
                y = ys[t % YB]
                if t == 0:
                    pe.wait_ge(bias_ready, b + 1)
                pe.wait_ge(y_free, NJ * b + before(t, YB) + 1 + CREDIT)
                mm(y[:, :], rows_on[:, 0, :], bias[:, q, :], start=True, stop=False, skip_group_check=True)
                for k in range(KD):
                    if t == 0 and k % 2 == 0:
                        pe.wait_ge(wtl_ready, 2 * b + k // 2 + 1)
                    ins = split_product(y[:, :], (
                        (x2h[q][:, k, blk(t)], wth[:, k, :]), (x2h[q][:, k, blk(t)], wtl[:, k, :]),
                        (x2l[q][:, k, blk(t)], wth[:, k, :])), False, k == KD - 1)
                ins.then_inc(y_ps, 1)

            def adapter_up(b, q, t):
                y = ys[t % YB]
                pe.wait_ge(x3_ready, NJ * b + t + 1)
                if t == 0:
                    pe.wait_ge(wul_ready, b + 1)
                if t % (NJ // 2) == 0:
                    pe.wait_ge(zl_ready, 2 * b + t // (NJ // 2) + 1)
                mm(y[:, :], rows_on[:, 1, :], bias[:, q, :], start=False, stop=False, skip_group_check=True)
                ins = split_product(y[:, :], (
                    (zh[:, blk(t)], wuh[:, q, :]), (zh[:, blk(t)], wul[:, q, :]),
                    (zl[:, blk(t)], wuh[:, q, :])), False, True)
                ins.then_inc(u_ps, 1)

            def program(b, n, m, q):
                if n is not None:
                    transpose_alpha(n)
                    transpose_p(n, 1)
                if b is not None:
                    adapter_up(b, 1 - q, 3)
                if n is not None:
                    pool_blocks(n, 0, (0,))
                    pool_blocks(n, 0, (1,))
                    pool_blocks(n, 0, (2,))
                if b is not None:
                    linear(b, 1 - q, 4)
                if n is not None:
                    pool_blocks(n, 1, (0, 1))
                    pool_blocks(n, 1, (2,))
                    pool_blocks(n, 2, (0, 1))
                if b is not None:
                    adapter_up(b, 1 - q, 4)
                if n is not None:
                    pool_blocks(n, 2, (2,))
                if b is not None:
                    linear(b, 1 - q, 5)
                if n is not None:
                    pool_blocks(n, 3, (0, 1))
                    pool_blocks(n, 3, (2,))
                if b is not None:
                    linear(b, 1 - q, 6)
                    linear(b, 1 - q, 7)
                    adapter_up(b, 1 - q, 5)
                    adapter_up(b, 1 - q, 6)
                    adapter_up(b, 1 - q, 7)
                if n is not None:
                    adapter_down(n, q, 0)
                    adapter_down(n, q, 1)
                    transpose_w(n, 0)
                    transpose_w(n, 1)
                    linear(n, q, 0)
                if m is not None:
                    transpose_x1(m, 0)
                    transpose_x1(m, 1)
                if n is not None:
                    linear(n, q, 1)
                if m is not None:
                    transpose_x1(m, 2)
                    score_hidden(m, 1 - q, 0)
                    transpose_x1(m, 3)
                if n is not None:
                    adapter_up(n, q, 0)
                    adapter_up(n, q, 1)
                if m is not None:
                    score_hidden(m, 1 - q, 1)
                    spread_scores(m, 0)
                    spread_scores(m, 1)
                    scores_by_row(m)
                    down_through_w(m)
                    block_sums(m)
                if n is not None:
                    linear(n, q, 2)
                    linear(n, q, 3)
                    adapter_up(n, q, 2)
                if m is not None:
                    transpose_p(m, 0)

            pe.wait_ge(const_made, CONST_MADE)
            pe.wait_ge(table_made, 1)
            run(pe, program)

        @block.scalar
        def _(act):
            def copy(dst, src):
                return act.activation(dst, src, ACT.Identity)

            def reflect(m, c):
                sl = c % 2
                act.wait_ge(x_loaded[sl], x_count(m, c))
                copy(xn[:, sl, :, 0:D + 2:D + 1], xn[:, sl, :, 2:D:D - 3]).then_inc(halo, 1)

            def scale_rows(m, c):
                sl = c % 2
                act.wait_ge(cur_ready, m + 1)
                act.wait_ge(pool_b, NC * m + c + 1)
                act.activation(xu[:, sl, :, :], xu[:, sl, :, :], ACT.Identity,
                               scale=cur[:, Z_Y:Z_Y + 1]).then_inc(scaled_rows, 1)

            def centre(m, c):
                sl = c % 2
                act.wait_ge(around, NC * m + c + 1)
                act.activation(xd[:, sl, :, :], xn[:, sl, :, 1:D + 1], ACT.Identity,
                               bias=cur[:, CENTRE:CENTRE + 1], scale=cur[:, MINUS_R:MINUS_R + 1]
                               ).then_inc(c_done, 1)

            def keep_x1t(n, q, c):
                act.wait_ge(xt_ps, NC * n + c + 1)
                wait_past(act, y_ps, NJ * (n - 1))
                pair = (pair_b, pair_a)[c % 2]
                copy(x1t[q][:, :, c * 2 * P:(c + 1) * 2 * P],
                     pair[:, :].rearrange("p (k q) -> p k q", k=KD)).then_inc(x1t_ready, 1)

            def hidden(n, h):
                wait_past(act, p_mm, KD * n)
                act.wait_ge(h_ps, 2 * n + h + 1)
                act.activation(th[:, half(h)], hidden_ps[h], ACT.Tanh,
                               bias=b1_col[:, 0:1]).then_inc(th_ready, 1)

            def small_exps(n):
                act.wait_ge(arg_ready, n + 1)
                wait_past(act, g_ps, n)
                act.activation(EX, ARG, ACT.Exp).then_inc(ex_ready, 1)

            def row_exps(n):
                act.wait_ge(negm_ready, n + 1)
                for j in range(NJ):
                    ins = act.activation(pn[:, blk(j)], pn[:, blk(j)], ACT.Exp, bias=NEGM[:, j:j + 1],
                                         accum_out=ZD[:, j:j + 1])
                ins.then_inc(p_exp, 1)

            def round_v(n):
                act.wait_ge(v_ps, n + 1)
                wait_past(act, z_ps, 2 * n)
                copy(vh[:, :, :], pair_a[:, 0:KD * P].rearrange("p (k q) -> p k q", k=KD)
                     ).then_inc(vh_ready, 1)

            def round_w(n, q):
                act.wait_ge(wt_ps, 2 * n + q + 1)
                wait_past(act, y_ps, NJ * n)
                copy(wth[:, 2 * q:2 * q + 2, :], (pair_b, pair_a)[q].rearrange(
                    "p (k q) -> p k q", k=2)).then_inc(wth_ready, 1)

            def round_up(n, q):
                act.wait_ge(up_loaded, 16 * n + 16)
                wait_past(act, y_free, NJ * (n - 1) + CREDIT)
                copy(wuh[:, q, :], wu[:, :]).then_inc(wuh_ready, 1)

            def round_bias(n, q):
                act.wait_ge(row_loaded, 96 * n + 96)
                wait_past(act, y_free, NJ * (n - 1) + CREDIT)
                copy(bias[:, q, :], rows[:, :]).then_inc(bias_h, 1)

            def keep_p(n, h):
                act.wait_ge(pt_ps, 2 * n + h + 1)
                if h == 0:
                    copy(pt[:, :, P], E_ROW)
                copy(pt[:, 4 * h:4 * h + 4, 0:P], pair_a[:, half(h)].rearrange("p (j l) -> p j l", l=P)
                     ).then_inc(pt_ready, 1)

            def keep_alpha(n):
                act.wait_ge(al_ps, n + 1)
                wait_past(act, x2s, KD * NG * n)
                copy(alb[:, :], pair_b[:, :]).then_inc(alb_ready, 1)

            def round_x2(n, q, k):
                act.wait_ge(x2s, NG * (KD * n + k + 1))
                copy(x2h[q][:, k, :], x2f[:, k % 2, :]).then_inc(x2h_ready, 1)

            def adapter_relu(n, h):
                act.wait_ge(bz_ready, n + 1)
                act.wait_ge(z_ps, 2 * n + h + 1)
                wait_past(act, u_ps, NJ * n - NJ // 2 + h * (NJ // 2))
                act.activation(zf[:, half(h)], pair_a[:, half(h)], ACT.Relu,
                               bias=bz[:, 0:1]).then_inc(zf_ready, 1)
                act.activation(zh[:, half(h)], pair_a[:, half(h)], ACT.Relu,
                               bias=bz[:, 0:1]).then_inc(zf_ready, 1)

            def keep_x3(b, t):
                act.wait_ge(y_ps, NJ * b + t + 1)
                act.wait_ge(fin_done, NJ * b + before(t, XB) + 1 + CREDIT)
                copy(x3[:, t % XB, :], ys[t % YB][:, :]).then_inc(x3_ready, 1)

            def scale(b, t):
                o = o_sb[:, t % OB, :]
                act.wait_ge(rstd_ready, NJ * b + t + 1)
                act.wait_ge(y_free, NJ * b + t + 1 + CREDIT)
                act.activation(o, o, ACT.Identity, scale=rstd[:, t % OB:t % OB + 1]).then_inc(scaled, 1)

            def store(b, t):
                act.wait_ge(fin_done, NJ * b + t + 1 + CREDIT)
                act.dma_start(out[bass.ds(b, 1), blk(t), :].rearrange("b p d -> p (b d)"),
                              o_sb[:, t % OB, :]).then_inc(stored[t % OB], 16)

            def program(b, n, m, q):
                if n is not None:
                    small_exps(n)
                    row_exps(n)
                    round_v(n)
                if b is not None:
                    keep_x3(b, 2)
                    keep_x3(b, 3)
                    scale(b, 1)
                if n is not None:
                    keep_p(n, 0)
                if m is not None:
                    reflect(m, 0)
                if n is not None:
                    keep_p(n, 1)
                    keep_alpha(n)
                if m is not None:
                    scale_rows(m, 0)
                    reflect(m, 1)
                if b is not None:
                    keep_x3(b, 4)
                if m is not None:
                    centre(m, 0)
                if b is not None:
                    store(b, 0)
                if n is not None:
                    round_x2(n, q, 0)
                if b is not None:
                    scale(b, 2)
                if n is not None:
                    round_x2(n, q, 1)
                if b is not None:
                    scale(b, 3)
                    store(b, 1)
                    scale(b, 4)
                    keep_x3(b, 5)
                if m is not None:
                    scale_rows(m, 1)
                if n is not None:
                    round_x2(n, q, 2)
                if b is not None:
                    store(b, 2)
                    keep_x3(b, 6)
                    store(b, 3)
                if n is not None:
                    round_x2(n, q, 3)
                if b is not None:
                    keep_x3(b, 7)
                if m is not None:
                    centre(m, 1)
                if n is not None:
                    adapter_relu(n, 0)
                if m is not None:
                    reflect(m, 2)
                if n is not None:
                    adapter_relu(n, 1)
                    round_w(n, 0)
                    round_w(n, 1)
                if m is not None:
                    scale_rows(m, 2)
                if b is not None:
                    scale(b, 5)
                if m is not None:
                    centre(m, 2)
                    reflect(m, 3)
                    scale_rows(m, 3)
                    keep_x1t(m, 1 - q, 0)
                if b is not None:
                    store(b, 4)
                if m is not None:
                    keep_x1t(m, 1 - q, 1)
                if b is not None:
                    scale(b, 6)
                    scale(b, 7)
                if m is not None:
                    centre(m, 3)
                if n is not None:
                    keep_x3(n, 0)
                    keep_x3(n, 1)
                if m is not None:
                    round_up(m, 1 - q)
                    keep_x1t(m, 1 - q, 2)
                if b is not None:
                    store(b, 5)
                if m is not None:
                    hidden(m, 0)
                if b is not None:
                    store(b, 6)
                if m is not None:
                    keep_x1t(m, 1 - q, 3)
                if b is not None:
                    store(b, 7)
                if n is not None:
                    scale(n, 0)
                if m is not None:
                    hidden(m, 1)
                    round_bias(m, 1 - q)

            act.wait_ge(const_in, 16 * CONST_DMAS)
            run(act, program)
            for q in range(OB):
                act.wait_ge(stored[q], 16 * (B * NJ // OB) + 16)

        @block.vector
        def _(dve):
            opening = Chain(dve_opening, 3)
            front = Chain(dve_front, 21)
            back = Chain(dve_back, NJ)

            def by_j(a):
                return a.rearrange("p (a b) -> p a b", b=NJ)

            def make_table():
                made = [0]

                def link(ins):
                    made[0] += 1
                    ins.then_inc(dve_setup, 1)
                    dve.wait_ge(dve_setup, made[0])

                link(dve.memset(rows[:, :], 0.0))
                link(dve.memset(rows_on_f[:, :, :], 0.0))
                for lo in (0, P // 2):
                    link(dve.memset(rows_on_f[lo:lo + 3, 0, :], 1.0))
                    link(dve.memset(rows_on_f[lo:lo + 1, 0, :], 0.0))
                    link(dve.memset(rows_on_f[lo:lo + 2, 1, :], -1.0))
                    link(dve.memset(rows_on_f[lo:lo + 1, 1, :], 1.0))
                link(dve.tensor_copy(rows_on[:, :, :], rows_on_f[:, :, :]))
                dve.wait_ge(const_in, 16 * CONST_DMAS)
                zx, zy, zr = (raw3[:, q, :] for q in range(3))
                link(dve.tensor_copy(tok_f[:, :], tok_i[:, :]))
                link(dve.tensor_copy(table[:, Z_X:Z_Y + 1, :], raw3[:, 0:2, :]))
                link(dve.tensor_scalar(table[:, MINUS_R, :], zr, -1.0, None, ALU.mult))
                link(dve.tensor_scalar(table[:, IS_PREFIX, :], tok_f[:, :], 0.0, None, ALU.is_equal))
                link(dve.tensor_scalar(table[:, IS_POSTFIX, :], tok_f[:, :], 1.0, None, ALU.is_equal))
                centre, cloze = table[:, CENTRE, :], table[:, IS_CLOZE, :]
                link(dve.tensor_scalar(centre, zx, -2.0, 1.0, ALU.mult, ALU.add))
                link(dve.scalar_tensor_tensor(out=centre, in0=zy, scalar=-2.0, in1=centre,
                                              op0=ALU.mult, op1=ALU.add))
                link(dve.tensor_tensor(centre, centre, zr, ALU.add))
                link(dve.tensor_scalar(cloze, table[:, IS_PREFIX, :], -1.0, 1.0, ALU.mult, ALU.add))
                dve.tensor_tensor(cloze, cloze, table[:, IS_POSTFIX, :], ALU.subtract).then_inc(table_made, 1)
                dve.wait_ge(table_made, 1)
                dve.wait_ge(const_made, CONST_MADE)

            def take_scalars(n):
                opening.start()
                wait_past(dve, c_done, NC * n)
                dve.tensor_copy(cur[:, :], table[:, :, bass.ds(n, 1)].rearrange("p a b -> p (a b)")
                                ).then_inc(cur_ready, 1)
                dve.wait_ge(cur_ready, n + 1)
                opening.mark(dve.tensor_scalar(mask[:, :], masks[:, 2, :], cur[:, IS_CLOZE:IS_CLOZE + 1],
                                             None, ALU.mult))
                for kind, col in ((1, IS_POSTFIX), (0, IS_PREFIX)):
                    opening.wait(dve, n)
                    opening.mark(dve.scalar_tensor_tensor(
                        out=mask[:, :], in0=masks[:, kind, :], scalar=cur[:, col:col + 1],
                        in1=mask[:, :], op0=ALU.mult, op1=ALU.add))

            def add_around(m, c):
                sl = c % 2
                dve.wait_ge(scaled_rows, NC * m + c + 1)
                dve.wait_ge(pool_a, NC * m + c + 1)
                dve.scalar_tensor_tensor(out=xu[:, sl, :, :], in0=xd[:, sl, :, :], scalar=cur[:, Z_X:Z_X + 1],
                                         in1=xu[:, sl, :, :], op0=ALU.mult, op1=ALU.add
                                         ).then_inc(around, 1)

            def times_x(m, c):
                sl = c % 2
                dve.wait_ge(c_done, NC * m + c + 1)
                dve.tensor_tensor(xd[:, sl, :, :], xd[:, sl, :, :], xn[:, sl, :, 1:D + 1],
                                  ALU.mult).then_inc(own_done, 1)

            def diffuse(m, c):
                dve.wait_ge(own_done, NC * m + c + 1)
                wait_past(dve, p_mm, KD * m)
                dve.tensor_tensor(x1[:, 2 * c:2 * c + 2, :], xd[:, c % 2, :, :], xu[:, c % 2, :, :],
                                  ALU.add).then_inc(l0_done, 1)

            def add_identity(n):
                dve.wait_ge(wt_loaded, 64 * n + 64)
                diagonal = wn[:, :, :].rearrange("p k h -> p (k h)")
                for k in range(KD):
                    d = diagonal[:, k * (D + P):k * (D + P) + P]
                    ins = dve.tensor_tensor(d, d, ident[:, :], ALU.add)
                ins.then_inc(wn_ready, 1)

            def mask_scores(n, h):
                if h == 0:
                    dve.wait_ge(dve_opening, opening.per_batch * n + opening.per_batch)
                wait_past(dve, pt_ps, 2 * n)
                spread = pair_b[:, half(h)].rearrange("p (j l) -> p j l", l=P)
                own_mask = mask[:, 0:P].rearrange("p (o l) -> p o l", o=1).to_broadcast([P, NJ // 2, P])
                dve.wait_ge(sc_ps, 2 * n + h + 1)
                if h == 0:
                    front.start()
                front.mark(dve.tensor_tensor(pn[:, half(h)].rearrange("p (j l) -> p j l", l=P),
                                             spread, own_mask, ALU.add))
                dve.tensor_reduce(MI[:, 4 * h:4 * h + 4], spread, AX.X, ALU.max).then_inc(sb_read, 1)

            def maxima(n):
                front.wait(dve, n)
                front.mark(dve.tensor_reduce(MDIAG, pn[:, :].rearrange("p (j l) -> p j l", l=P),
                                             AX.X, ALU.max))
                dve.wait_ge(sb_read, 2 * n + 2)
                mi_all = MI.rearrange("p (o i) -> p o i", o=1).to_broadcast([P, NJ, NJ])
                front.mark(dve.tensor_tensor(by_j(KM), by_j(mask[:, P:P + NB]), mi_all, ALU.add))
                front.wait(dve, n)
                front.mark(dve.tensor_reduce(MCAR, by_j(KM), AX.X, ALU.max))
                dve.wait_ge(sn_ps, n + 1)
                front.mark(dve.tensor_tensor(ARG[:, 0:NJ], SN, MI, ALU.subtract))
                front.wait(dve, n)
                front.mark(dve.tensor_tensor(M, MDIAG, MCAR, ALU.max))
                mcar_all = MCAR.rearrange("p (j o) -> p j o", o=1).to_broadcast([P, NJ, NJ])
                front.mark(dve.tensor_tensor(by_j(ARG[:, NJ:NJ + NB]), by_j(KM), mcar_all, ALU.subtract))
                front.wait(dve, n)
                wait_past(dve, p_exp, n)
                dve.tensor_scalar(NEGM, M, -1.0, None, ALU.mult).then_inc(negm_ready, 1)
                dve.tensor_tensor(ARG[:, NJ + NB:], MCAR, M, ALU.subtract).then_inc(arg_ready, 1)

            def rest_v(n):
                dve.wait_ge(vh_ready, n + 1)
                dve.tensor_tensor(vl[:, :, :], pair_a[:, 0:KD * P].rearrange("p (k q) -> p k q", k=KD),
                                  vh[:, :, :].bitcast(F32), ALU.subtract).then_inc(vl_ready, 1)

            def block_weights(n):
                dve.wait_ge(g_ps, n + 1)
                dve.wait_ge(ex_ready, n + 1)
                front.mark(dve.tensor_tensor(prod[:, 0, :, :], ZG.rearrange("p (o i) -> p o i", o=1
                                             ).to_broadcast([P, NJ, NJ]), by_j(KAP), ALU.mult))
                front.wait(dve, n)
                dve.tensor_reduce(CC[:, 0:NJ], prod[:, 0, :, :], AX.X, ALU.add).then_inc(cc_ready, 1)

            def row_weights(n):
                dve.wait_ge(cc_ready, n + 1)
                front.mark(dve.tensor_tensor(ZT, ALH, CC[:, 0:NJ], ALU.mult))
                dve.wait_ge(p_exp, n + 1)
                front.wait(dve, n)
                front.mark(dve.tensor_tensor(ZT2, ZT, ZD, ALU.add))
                front.wait(dve, n)
                front.mark(dve.tensor_tensor(ZT, ZT2, mask[:, P + NB:MASK], ALU.mult))
                front.wait(dve, n)
                front.mark(dve.reciprocal(RZ, ZT))
                front.wait(dve, n)
                wait_past(dve, al_ps, n)
                dve.tensor_tensor(AL, ALH, RZ, ALU.mult).then_inc(al_ready, 1)

            def probabilities(n, h):
                for j in range(4 * h, 4 * h + 4):
                    ins = dve.scalar_tensor_tensor(out=pn[:, blk(j)], in0=pn[:, blk(j)],
                                                   scalar=RZ[:, j:j + 1], in1=ident[:, :],
                                                   op0=ALU.mult, op1=ALU.add)
                ins.then_inc(pn_ready, 1)

            def adapter_bias(n):
                dve.wait_ge(bz_ps, n + 1)
                wait_past(dve, zf_ready, 4 * n)
                dve.tensor_tensor(bz[:, :], BZ, bd_col[:, :], ALU.add).then_inc(bz_ready, 1)

            def rest_w(n, q):
                dve.wait_ge(wth_ready, 2 * n + q + 1)
                dve.tensor_tensor(wtl[:, 2 * q:2 * q + 2, :], (pair_b, pair_a)[q].rearrange(
                    "p (k q) -> p k q", k=2), wth[:, 2 * q:2 * q + 2, :].bitcast(F32),
                    ALU.subtract).then_inc(wtl_ready, 1)

            def carry_products(n, k):
                dve.wait_ge(p_mm, KD * n + k + 1)
                for g, (j0, j1) in enumerate(GROUPS):
                    sums = front_ps[:, GROUP_BANK[k % 2][g], 0:(j1 - j0) * (P + 1)].rearrange(
                        "p (o i c) -> p o i c", o=1, c=P + 1)[:, :, :, P]
                    ins = dve.tensor_tensor(prod[:, k % 2, :, j0:j1], sums.to_broadcast([P, NJ, j1 - j0]),
                                            by_j(KAP)[:, :, j0:j1], ALU.mult)
                front.mark(ins)

            def carry(k):
                return CC[:, (k + 1) * NJ:(k + 2) * NJ]

            def carry_sums(n, k):
                front.wait(dve, n)
                front.mark(dve.tensor_reduce(carry(k), prod[:, k % 2, :, :], AX.X, ALU.add))

            def add_carry(n, k, g):
                if g == GROUP_ORDER[0]:
                    wait_past(dve, x2h_ready, KD * n + k - 1)
                    wait_past(dve, x2l_ready, KD * n + k - 1)
                    if k == 0:
                        dve.wait_ge(alb_ready, n + 1)
                        wait_past(dve, zl_ready, 2 * n)
                    front.wait(dve, n)
                j0, j1 = GROUPS[g]
                for j in range(j0, j1):
                    o = (j - j0) * (P + 1)
                    ins = dve.scalar_tensor_tensor(
                        out=x2f[:, k % 2, blk(j)], in0=alb[:, blk(j)], scalar=carry(k)[:, j:j + 1],
                        in1=front_ps[:, GROUP_BANK[k % 2][g], o:o + P], op0=ALU.mult, op1=ALU.add)
                ins.then_inc(x2s, 1)

            def rest_z(n, h):
                dve.wait_ge(zf_ready, 4 * n + 2 * h + 2)
                dve.tensor_tensor(zl[:, half(h)], zf[:, half(h)], zh[:, half(h)].bitcast(F32),
                                  ALU.subtract).then_inc(zl_ready, 1)

            def moments(b, t):
                r = t % OB
                if t == 0:
                    back.start()
                dve.wait_ge(u_ps, NJ * b + t + 1)
                back.mark(dve.bn_stats(stats[:, r, :], ys[t % YB][:, :]))
                back.wait(dve, b)
                dve.memset(carrier[:, :], 0.0)
                dve.bn_aggr(mv[:, r, :], stats[:, r, :]).then_inc(mv_ready, 1)
                dve.wait_ge(mv_ready, NJ * b + t + 1)
                dve.wait_ge(stored[t % OB], 16 * (NJ // OB * b + t // OB) + 16)
                dve.tensor_scalar(ve[:, r:r + 1], mv[:, r, 1:2], EPS, None, ALU.add).then_inc(ve_ready, 1)

            def subtract_mean(b, q, t):
                dve.wait_ge(g_loaded, 16 * b + 16)
                dve.scalar_tensor_tensor(out=o_sb[:, t % OB, :], in0=ys[t % YB][:, :],
                                         scalar=mv[:, t % OB, 0:1], in1=g_row[:, q, :],
                                         op0=ALU.subtract, op1=ALU.mult).then_inc(y_free, 1)

            def program(b, n, m, q):
                if n is not None:
                    maxima(n)
                if b is not None:
                    moments(b, 1)
                if n is not None:
                    block_weights(n)
                if b is not None:
                    subtract_mean(b, 1 - q, 1)
                if n is not None:
                    row_weights(n)
                    probabilities(n, 0)
                    rest_v(n)
                    adapter_bias(n)
                    probabilities(n, 1)
                if b is not None:
                    moments(b, 2)
                if m is not None:
                    take_scalars(m)
                if b is not None:
                    moments(b, 3)
                if n is not None:
                    carry_products(n, 0)
                if b is not None:
                    subtract_mean(b, 1 - q, 2)
                if n is not None:
                    carry_sums(n, 0)
                if m is not None:
                    add_around(m, 0)
                if n is not None:
                    add_carry(n, 0, 2)
                    add_carry(n, 0, 0)
                    add_carry(n, 0, 1)
                    carry_products(n, 1)
                    carry_sums(n, 1)
                    add_carry(n, 1, 2)
                    add_carry(n, 1, 0)
                if b is not None:
                    subtract_mean(b, 1 - q, 3)
                if n is not None:
                    carry_products(n, 2)
                    add_carry(n, 1, 1)
                    carry_sums(n, 2)
                if b is not None:
                    moments(b, 4)
                if n is not None:
                    add_carry(n, 2, 2)
                if m is not None:
                    times_x(m, 0)
                if b is not None:
                    subtract_mean(b, 1 - q, 4)
                if n is not None:
                    carry_products(n, 3)
                    add_carry(n, 2, 0)
                    carry_sums(n, 3)
                    add_carry(n, 2, 1)
                    add_carry(n, 3, 2)
                    add_carry(n, 3, 0)
                    add_carry(n, 3, 1)
                if m is not None:
                    diffuse(m, 0)
                    add_around(m, 1)
                if b is not None:
                    moments(b, 5)
                if m is not None:
                    times_x(m, 1)
                    diffuse(m, 1)
                if b is not None:
                    moments(b, 6)
                    subtract_mean(b, 1 - q, 5)
                    subtract_mean(b, 1 - q, 6)
                    moments(b, 7)
                if n is not None:
                    rest_w(n, 0)
                    rest_w(n, 1)
                if m is not None:
                    add_around(m, 2)
                if n is not None:
                    rest_z(n, 0)
                if b is not None:
                    subtract_mean(b, 1 - q, 7)
                if m is not None:
                    times_x(m, 2)
                    diffuse(m, 2)
                    add_around(m, 3)
                if n is not None:
                    rest_z(n, 1)
                if m is not None:
                    add_identity(m)
                    times_x(m, 3)
                    diffuse(m, 3)
                if n is not None:
                    moments(n, 0)
                    subtract_mean(n, q, 0)
                if m is not None:
                    mask_scores(m, 0)
                    mask_scores(m, 1)

            dve.sem_inc(y_free, CREDIT)
            dve.sem_inc(fin_done, CREDIT)
            for slot in range(OB):
                dve.sem_inc(stored[slot], 16)
            make_table()
            run(dve, program)


_INS = ["x", "condB_zX", "condB_zY", "condB_zR", "itok_B_0_2", "itok_B_0_7", "itok_B_0_6",
        "L1_cond_W1", "L1_cond_b1", "L1_cond_v", "L2_cond_weight", "L2_cond_bias", "L3_cond_down_w",
        "L3_cond_down_b", "L3_cond_up_w", "L3_cond_up_b", "L3_cond_ln_g", "L3_cond_ln_b"]


def kernel(**inputs):
    import concourse.bacc as bacc
    from concourse.bass_utils import run_bass_kernel_spmd

    nc = bacc.Bacc("TRN2", target_bir_lowering=False, num_devices=1)
    arrays, args = {}, []
    for name in _INS:
        a = np.ascontiguousarray(inputs[name])
        arrays[f"in_{name}"] = a
        args.append(nc.dram_tensor(f"in_{name}", a.shape, mybir.dt.from_np(a.dtype),
                                   kind="ExternalInput").ap())
    out = nc.dram_tensor("out_0", inputs["x"].shape, F32, kind="ExternalOutput").ap()
    build(nc, *args, out)
    return run_bass_kernel_spmd(nc, [arrays], core_ids=[0]).results[0]["out_0"]
```
